# Optimizing a Trainium2 kernel written in Bass

```python
import numpy as np
import jax
import jax.numpy as jnp

def _softmax(x, axis=-1):
    return jax.nn.softmax(x, axis=axis)

def _gelu(x):
    return jax.nn.gelu(x, approximate=True)

def _silu(x):
    return jax.nn.silu(x)

def _sigmoid(x):
    return jax.nn.sigmoid(x)

def _layernorm(x, axis=-1, eps=1e-05):
    m = jnp.mean(x, axis=axis, keepdims=True)
    v = jnp.var(x, axis=axis, keepdims=True)
    return (x - m) / jnp.sqrt(v + eps)

def _scatter_add(tgt, idx, src, axis=0):
    return tgt.at[idx].add(src)

def _segment_sum(src, seg, n):
    return jax.ops.segment_sum(src, seg, n)
kernel_name = 'mk_flamingo_gated_d1_seqx_r8_0a4924'

def setup_inputs(seed: int=0):
    np.random.seed(seed)
    _w = jnp.asarray

    def _rec_inputs():
        import jax
        import jax.numpy as jnp
        _rk = jax.random.key(seed)
        x = 7.22e-05 + 1 * jax.random.normal(jax.random.fold_in(_rk, 1), (8, 128, 256), jnp.float32)
        _lenS = 128 - jax.random.randint(jax.random.fold_in(_rk, 7), (8,), 0, max(1, 128 // 4) + 1, jnp.int32)
        _lenS2 = 128 - jax.random.randint(jax.random.fold_in(_rk, 8), (8,), 0, max(1, 128 // 4) + 1, jnp.int32)
        _ctx_512P = jax.random.normal(jax.random.fold_in(_rk, 11), (8, 16, 64), jnp.float32)
        _ctx_512c = jax.random.dirichlet(jax.random.fold_in(_rk, 511), 0.3 * jnp.ones((16,), jnp.float32), (8, 128))
        _ctx_512t = jnp.einsum('bsk,bkd->bsd', _ctx_512c, _ctx_512P)
        _ctx_512t = _ctx_512t * jax.lax.rsqrt(jnp.mean(jnp.square(_ctx_512t)) + 1e-12) * 0.953939
        ctx_512 = -0.000514642 + 1.00011 * (_ctx_512t + 0.3 * jax.random.normal(jax.random.fold_in(_rk, 611), (8, 128, 64), jnp.float32))
        _g = jax.random.normal(jax.random.fold_in(_rk, 9001), (2, 1), jnp.float32)
        _g = jnp.sign(_g) * jnp.maximum(jnp.abs(_g), 1.0) + (_g == 0) * 1.0
        g_xattn = _g[0]
        g_ffn = _g[1]
        return (x, ctx_512, g_xattn, g_ffn)
    x, ctx_512, g_xattn, g_ffn = _rec_inputs()

    def _L0_xattn_setup():
        import jax, jax.numpy as jnp
        import numpy as np
        B, S, H, NH, L = (2, 256, 256, 16, 64)
        HD = H // NH
        key = jax.random.key(seed)
        k1, k2, k3, k4, k5 = jax.random.split(key, 5)
        scale = 0.02
        return {'q': jax.random.normal(k1, (B, S, H), dtype=jnp.float32), 'latent_kv': jax.random.normal(k2, (B, S, L), dtype=jnp.float32), 'Wq': jax.random.normal(k3, (H, H), dtype=jnp.float32) * scale, 'Wkv_expand': jax.random.normal(k4, (2 * H, L), dtype=jnp.float32) * scale, 'Wout': jax.random.normal(k5, (H, H), dtype=jnp.float32) * scale}
    _L0_xattn_all = _L0_xattn_setup()
    _L0_xattn_in = {k: v for k, v in _L0_xattn_all.items() if k in ('Wq', 'Wkv_expand', 'Wout')}
    del _L0_xattn_all

    def _L0_ffn_setup():
        import jax, jax.numpy as jnp
        import numpy as np
        B, T, D = (4, 256, 256)
        E = 8
        K = 2
        F = 1024 // (E // 2)
        key = jax.random.key(seed)
        ks = jax.random.split(key, 5)
        s_in = 1.0 / np.sqrt(D)
        s_mid = 1.0 / np.sqrt(F)
        x = jax.random.normal(ks[0], (B, T, D), dtype=jnp.float32)
        Wr = jax.random.normal(ks[1], (D, E), dtype=jnp.float32) * s_in
        Wg = jax.random.normal(ks[2], (E, D, F), dtype=jnp.float32) * s_in
        Wu = jax.random.normal(ks[3], (E, D, F), dtype=jnp.float32) * s_in
        Wd = jax.random.normal(ks[4], (E, F, D), dtype=jnp.float32) * s_mid
        return {'x': x, 'Wr': Wr, 'Wg': Wg, 'Wu': Wu, 'Wd': Wd}
    _L0_ffn_all = _L0_ffn_setup()
    _L0_ffn_in = {k: v for k, v in _L0_ffn_all.items() if k in ('Wr', 'Wg', 'Wu', 'Wd')}
    del _L0_ffn_all
    return {'x': x, 'ctx_512': ctx_512, 'g_xattn': g_xattn, 'g_ffn': g_ffn, 'L0_xattn_Wq': _L0_xattn_in['Wq'], 'L0_xattn_Wkv_expand': _L0_xattn_in['Wkv_expand'], 'L0_xattn_Wout': _L0_xattn_in['Wout'], 'L0_ffn_Wr': _L0_ffn_in['Wr'], 'L0_ffn_Wg': _L0_ffn_in['Wg'], 'L0_ffn_Wu': _L0_ffn_in['Wu'], 'L0_ffn_Wd': _L0_ffn_in['Wd']}

def reference(x, ctx_512, g_xattn, g_ffn, L0_xattn_Wq, L0_xattn_Wkv_expand, L0_xattn_Wout, L0_ffn_Wr, L0_ffn_Wg, L0_ffn_Wu, L0_ffn_Wd):
    import jax
    import jax.numpy as jnp

    def _L0_xattn_ref(q, latent_kv, Wq, Wkv_expand, Wout):
        import jax, jax.numpy as jnp
        import numpy as np
        B, S, H, NH, L = (2, 256, 256, 16, 64)
        HD = H // NH
        b, sq, _ = q.shape
        sk = latent_kv.shape[1]
        qp = q @ Wq.T
        kv = latent_kv @ Wkv_expand.T
        k, v = jnp.split(kv, 2, axis=-1)
        qh = qp.reshape(b, sq, NH, HD).transpose(0, 2, 1, 3)
        kh = k.reshape(b, sk, NH, HD).transpose(0, 2, 1, 3)
        vh = v.reshape(b, sk, NH, HD).transpose(0, 2, 1, 3)
        inv_sqrt_d = 1.0 / jnp.sqrt(jnp.float32(HD))
        scores = jnp.einsum('bhqd,bhkd->bhqk', qh, kh) * inv_sqrt_d
        causal = jnp.tril(jnp.ones((sq, sk), dtype=bool))
        scores = jnp.where(causal, scores, jnp.finfo(scores.dtype).min)
        attn = jax.nn.softmax(scores, axis=-1)
        out = jnp.einsum('bhqk,bhkd->bhqd', attn, vh)
        out = out.transpose(0, 2, 1, 3).reshape(b, sq, H)
        return out @ Wout.T

    def _L0_ffn_ref(x, Wr, Wg, Wu, Wd):
        import jax, jax.numpy as jnp
        import numpy as np
        B, T, D = (4, 256, 256)
        E = 8
        K = 2
        F = 1024 // (E // 2)
        probs = jax.nn.softmax(x @ Wr, axis=-1)
        topk_w, topk_idx = jax.lax.top_k(probs, K)
        topk_w = topk_w / jnp.sum(topk_w, axis=-1, keepdims=True)
        output = jnp.zeros_like(x)
        for i in range(E):
            sel = topk_idx == i
            w_i = jnp.sum(topk_w * sel.astype(x.dtype), axis=-1, keepdims=True)
            h = jax.nn.silu(x @ Wg[i]) * (x @ Wu[i])
            e_out = h @ Wd[i]
            output = output + w_i * e_out
        return output
    x = x + jnp.tanh(g_xattn[0]) * _L0_xattn_ref(_layernorm(x, axis=-1), ctx_512, L0_xattn_Wq, L0_xattn_Wkv_expand, L0_xattn_Wout)
    x = x + jnp.tanh(g_ffn[0]) * _L0_ffn_ref(_layernorm(x, axis=-1), L0_ffn_Wr, L0_ffn_Wg, L0_ffn_Wu, L0_ffn_Wd)
    return x

_drawn_inputs = setup_inputs


def setup_inputs(seed=0):
    import zlib

    import numpy as np

    out = dict(_drawn_inputs(seed))
    spreads = {}
    factors = {'L0_xattn_Wq': 39.376}
    for name, (base, spread) in spreads.items():
        noise = np.random.default_rng([zlib.crc32(name.encode()), seed]).standard_normal(out[name].shape)
        drawn = base * np.exp(spread * noise) if base else spread * noise
        out[name] = jnp.asarray(drawn.astype(out[name].dtype))
    for name, factor in factors.items():
        out[name] = (out[name] * factor).astype(out[name].dtype)
    return out
```

```python
from contextlib import ExitStack

import concourse.bass as bass
from concourse import mybir

ALU = mybir.AluOpType
ACT = mybir.ActivationFunctionType
AX_X = mybir.AxisListType.X
F32 = mybir.dt.float32
F32R = mybir.dt.float32r
BF16 = mybir.dt.bfloat16
F16 = mybir.dt.float16

P = 128


def build_gated_block(nc, x, ctxT, g_attn, g_ffn, WqT, WkvT, WoT, Wr, Wgu, Wd, out):
    NTOK, D = x.shape
    L = ctxT.shape[0]
    NB = NTOK // P
    KC = D // P
    HD = 16
    NH = D // HD
    HPC = P // HD
    E, _, F2 = Wgu.shape
    GH = 4
    GPB = NH // GH
    NG = NB * GPB
    SLOTS = 2 * GPB
    VW = 3 * HD + 2
    BANK = 512
    WPE = KC * F2 + KC * D
    PIECE = 512
    PIECES = WPE // PIECE
    EARLY = 4
    QSCALE = HD ** -0.5
    PSCALE = 4096.0
    MASKED = -3.0e38
    EPS = 1e-5
    assert L * 2 == P and D == KC * P and F2 == 2 * D and NB == 8 and E == 8

    with ExitStack() as ctx:
        def sb(name, shape, dt=F32):
            return ctx.enter_context(nc.sbuf_tensor(name, shape, dt))

        def sem(name):
            return ctx.enter_context(nc.semaphore(name))

        ps = ctx.enter_context(nc.psum_tensor("ps", [P, 8, BANK], F32))

        xs = sb("xs", [P, NB, D])
        nrm = sb("nrm", [P, 4, D])
        xT = sb("xT", [P, 2, KC, NTOK], F32R)
        kbd = sb("kbd", [P, 2, 4, HPC, P], F32R)
        qb = sb("qb", [P, 2, 4, P], F32R)
        vx = sb("vx", [P, NB, NH, VW], BF16)
        W = sb("W", [P, E, 2, WPE], F32R)
        stage = sb("stage", [P, 2, WPE])
        prob = sb("prob", [P, 2, BANK])
        pth = sb("pth", [P, 2, BANK], F16)
        ptl = sb("ptl", [P, 2, BANK], F16)
        attr = sb("attr", [P, D])
        att = sb("att", [P, D])
        rT = sb("rT", [P, 2, 2, KC, P], F32R)
        wo = sb("wo", [P, 2, KC, D], F32R)
        wrr = sb("wrr", [P, KC, E])
        wr = sb("wr", [P, 2, KC, E], F32R)
        identf = sb("identf", [P, P])
        identb = sb("identb", [P, P], BF16)
        mask = sb("mask", [P, GH, P], BF16)
        stat = sb("stat", [P, NB, 6])
        mv = sb("mv", [P, NB, 2])
        rstd = sb("rstd", [P, NB, 1])
        junk = sb("junk", [P, D], BF16)
        mv2 = sb("mv2", [P, 2, 2])
        rstd2 = sb("rstd2", [P, 2, 1])
        mhalf = sb("mhalf", [P, NB, 1])
        one = sb("one", [P, 1])
        negm = sb("negm", [P, 2, GH])
        rinv = sb("rinv", [P, HPC])
        gate = sb("gate", [P, 2])
        tg = sb("tg", [P, 2])
        lg = sb("lg", [P, NB, E])
        lmax = sb("lmax", [P, NB])
        pr = sb("pr", [P, NB, E])
        psum_r = sb("psum_r", [P, NB])
        tri = sb("tri", [P, NB * E, E], BF16)
        rank = sb("rank", [P, NB, E])
        wtok = sb("wtok", [P, E, NB])

        late = W[:, EARLY:E, :, :].rearrange("p e h w -> p (e h w)")
        NQ = 4 * NTOK
        qT = late[:, 0:NQ].rearrange("p (a t) -> p a t", a=4)
        kT = late[:, NQ:2 * NQ].rearrange("p (a t) -> p a t", a=4)
        cT = late[:, 2 * NQ:2 * NQ + 2 * NTOK].rearrange("p (a t) -> p a t", a=2)
        at = 2 * NQ + 2 * NTOK
        wq = late[:, at:at + 2 * KC * D].rearrange("p (a c n) -> p a c n", a=2, c=KC)
        at += 2 * KC * D
        wkv = late[:, at:at + 2 * D]
        rawq = stage[:, 0, 0:512].rearrange("p (c n) -> p c n", c=KC)
        rawo = stage[:, 0, 512:1024].rearrange("p (c n) -> p c n", c=KC)
        rawkv = stage[:, 0, 1024:1536]
        rawc = stage[:, 1, 0:NTOK]
        vres = prob
        sg = prob
        h = nrm

        lgT = prob[0:E, :, :].rearrange("p a n -> p (a n)")
        cmp2 = vx[:, 0:NB // 2, :, :].rearrange("p b h w -> p (b h w)")[:, 0:4 * NB * E * E].bitcast(F32)
        cmpa, cmpb = (cmp2[:, NB * E * E * k:NB * E * E * (k + 1)].rearrange("p (t i j) -> p t i j", t=NB, i=E)
                      for k in range(2))

        def f(ap):
            return ap.bitcast(F32)

        in_x = [sem(f"in_x{i}") for i in range(2)]
        in_kv, in_c, in_q, in_o, in_g = (sem("in_" + n) for n in ("kv", "c", "q", "o", "g"))
        ident_set, identb_set, mask_set, ones_set, mhalf_set, kbd_zeroed = (
            sem(n) for n in ("ident_set", "identb_set", "mask_set", "ones_set", "mhalf_set", "kbd_zeroed"))
        ident_zero, mask_zero, tri_set = sem("ident_zero"), sem("mask_zero"), sem("tri_set")
        wkv_hi, wkv_split, c_hi, c_split = (sem(n) for n in ("wkv_hi", "wkv_split", "c_hi", "c_split"))
        wq_hi, wq_split, wo_hi, wo_split, wr_hi, wr_split = (
            sem(n) for n in ("wq_hi", "wq_split", "wo_hi", "wo_split", "wr_hi", "wr_split"))
        stats1, aggr1, eps1, rstd1, norm1 = (sem(n) for n in ("stats1", "aggr1", "eps1", "rstd1", "norm1"))
        job_done, job_hi, job_lo, v2_done, v3_done = (
            sem(n) for n in ("job_done", "job_hi", "job_lo", "v2_done", "v3_done"))
        tg_set = sem("tg_set")
        kq_loaded = [sem(f"kq_loaded{u}") for u in range(2)]
        scores_done, negm_done, exp_done, turned, pth_done, ptl_done, pv_done = (
            sem(n) for n in ("scores_done", "negm_done", "exp_done", "turned", "pth_done", "ptl_done", "pv_done"))
        sums_done, att_done, attT_done, attT_hi, attT_lo, oproj_done, x1_done = (
            sem(n) for n in ("sums_done", "att_done", "attT_done", "attT_hi", "attT_lo", "oproj_done", "x1_done"))
        mean2, centred2, squares2, eps2, rstd2_done, norm2, x2T_done, x2T_hi, x2T_lo = (
            sem(n) for n in ("mean2", "centred2", "squares2", "eps2", "rstd2_done", "norm2", "x2T_done", "x2T_hi", "x2T_lo"))
        in_w, w_hi, w_split = [sem("in_w0"), sem("in_w1")], sem("w_hi"), sem("w_split")
        rt_done, rt_out, rt_T, rt_step, rt_exp_in, rt_exp, w_ready = (
            sem(n) for n in ("rt_done", "rt_out", "rt_T", "rt_step", "rt_exp_in", "rt_exp", "w_ready"))
        gu_done, silu_done, h_done, hT_done, hT_hi, hT_lo, y_done, acc_done = (
            sem(n) for n in ("gu_done", "silu_done", "h_done", "hT_done", "hT_hi", "hT_lo", "y_done", "acc_done"))
        out_done = sem("out_done")

        x_v = x.rearrange("(b p) d -> p b d", p=P)
        out_v = out.rearrange("(b p) d -> p b d", p=P)
        TURN_LAG, EVICT_LAG, PV_LAG, HALF0_LAG, HALF1_LAG = 1, 2, 3, 5, 7
        ATT_T_LAG, ATT_LO_LAG, OPROJ_LAG, X1_LAG, POW_LAG, NORM2_LAG, X2T_LAG, X2T_OUT_LAG = 8, 8, 9, 9, 9, 10, 11, 11
        TAIL = X2T_OUT_LAG - GPB + 1
        PREFETCHES = 16 * (HPC + 1)

        def due(i, s, lag, step=1, last=NG):
            n = s - lag
            if n % step:
                return False
            return not isinstance(i, int) or 0 <= SLOTS * i + n < last

        def schedule(eng, body, iterations, tail):
            body(0, range(SLOTS))
            with eng.Fori(1, iterations) as i:
                body(i, range(SLOTS))
            body(iterations, range(tail))

        HALF = NTOK // 2
        JOBS = []
        for hf in range(2):
            JOBS += [("k", mc, hf) for mc in range(KC)] + [("t", 2 * hf, 0), ("t", 2 * hf + 1, 0)]
            JOBS += [("q", mc, hf) for mc in range(KC)] + [("v", 2 * hf, 0), ("v", 2 * hf + 1, 0)]
        HALF_JOBS = len(JOBS) // 2

        def job(kind, a, hf=0):
            return JOBS.index((kind, a, hf)) + 1

        block = ctx.enter_context(nc.Block())

        @block.sync
        def _(sp):
            sp.dma_start(xs[:, 0:NB // 2, :], x_v[:, 0:NB // 2, :]).then_inc(in_x[0], 16)
            for half in range(2):
                sp.dma_start(rawkv[L * half:L * half + L, :], WkvT).then_inc(in_kv, 16)
            for half in range(2):
                sp.dma_start(rawc[L * half:L * half + L, :], ctxT).then_inc(in_c, 16)
            sp.dma_start(xs[:, NB // 2:NB, :], x_v[:, NB // 2:NB, :]).then_inc(in_x[1], 16)
            sp.dma_start(rawq, WqT.rearrange("(c p) n -> p c n", p=P)).then_inc(in_q, 16)
            sp.dma_start(gate[:, 0:1], g_attn.partition_broadcast(P)).then_inc(in_g, 16)
            sp.dma_start(gate[:, 1:2], g_ffn.partition_broadcast(P)).then_inc(in_g, 16)
            sp.dma_start(rawo, WoT.rearrange("(c p) n -> p c n", p=P)).then_inc(in_o, 16)
            sp.dma_start(wrr[:, :, :], Wr.rearrange("(c p) n -> p c n", p=P)).then_inc(in_o, 16)
            sp.wait_ge(job_hi, job("q", KC - 1, 0))
            sp.wait_ge(job_lo, job("q", KC - 1, 0))
            sp.wait_ge(kbd_zeroed, 2)

            def prefetch(u, b):
                for j in range(HPC):
                    rows = slice(HD * j, HD * j + HD)
                    sp.dma_start(f(kbd[rows, u, :, j, :]), f(kT[rows, :, bass.ts(b, P)])).then_inc(kq_loaded[u], 16)
                sp.dma_start(f(qb[:, u, :, :]), f(qT[:, :, bass.ts(b, P)])).then_inc(kq_loaded[u], 16)

            def load_expert(e, slot):
                sp.dma_start(stage[:, slot, 0:KC * F2].rearrange("p (c n) -> p c n", c=KC),
                             Wgu[e].rearrange("(c p) n -> p c n", p=P)).then_inc(in_w[slot], 16)
                sp.dma_start(stage[:, slot, KC * F2:].rearrange("p (c n) -> p c n", c=KC),
                             Wd[e].rearrange("(c p) n -> p c n", p=P)).then_inc(in_w[slot], 16)

            prefetch(0, 0)
            prefetch(1, 1)
            sp.wait_ge(wq_split, 1)
            sp.wait_ge(wkv_split, 1)
            sp.wait_ge(wo_split, 1)
            load_expert(0, 0)
            sp.wait_ge(job_lo, len(JOBS))
            for i in range(1, EARLY):
                for u in range(2):
                    sp.wait_ge(scores_done, GPB * (2 * (i - 1) + u + 1))
                    prefetch(u, 2 * i + u)
                sp.wait_ge(w_split, PIECES * i)
                load_expert(i, 0)
            for u in range(2):
                sp.wait_ge(kq_loaded[u], PREFETCHES * (NB // 2))
            for e in range(EARLY, E):
                slot = (e - EARLY) % 2
                sp.wait_ge(w_split, PIECES * (EARLY if e < EARLY + 2 else e - 1))
                load_expert(e, slot)
            for t in range(NB):
                sp.wait_ge(acc_done, NB * (E - 1) + t + 1)
                sp.dma_start(out_v[:, t, :], xs[:, t, :]).then_inc(out_done, 16)
            sp.wait_ge(out_done, 16 * NB)

        @block.gpsimd
        def _(pool):
            def split(dst_hi, dst_lo, src, hi_sem, hi_count, lo_sem):
                nc.gpsimd.tensor_copy(dst_hi, src).then_inc(hi_sem, 1)
                pool.wait_ge(hi_sem, hi_count)
                nc.gpsimd.tensor_tensor(dst_lo, src, f(dst_hi), ALU.subtract).then_inc(lo_sem, 1)

            nc.gpsimd.memset(identf[:, :], 0.0).then_inc(ident_zero, 1)
            pool.wait_ge(ident_zero, 1)
            nc.gpsimd.affine_select(out=identf[:, :], in_=identf[:, :], compare_op=ALU.not_equal, fill=1.0, base=0,
                                    pattern=[[-1, P]], channel_multiplier=1).then_inc(ident_set, 1)
            nc.gpsimd.memset(mhalf[:, :, :], -0.5).then_inc(mhalf_set, 1)
            nc.gpsimd.memset(one[:, :], 1.0).then_inc(mhalf_set, 1)
            nc.gpsimd.memset(f(kbd[:, 1, :, :, :]), 0.0).then_inc(kbd_zeroed, 1)
            pool.wait_ge(in_kv, 32)
            nc.gpsimd.tensor_copy(wkv[:, :], rawkv).then_inc(wkv_hi, 1)
            pool.wait_ge(c_hi, 1)
            nc.gpsimd.tensor_tensor(cT[:, 1, :], rawc, f(cT[:, 0, :]), ALU.subtract).then_inc(c_split, 1)
            pool.wait_ge(eps1, 1)
            pool.wait_ge(mhalf_set, 2)
            nc.gpsimd.tensor_tensor(rstd[:, :, :], mv[:, :, 1:2], mhalf[:, :, :], ALU.pow).then_inc(rstd1, 1)
            pool.wait_ge(in_q, 16)
            split(wq[:, 0], wq[:, 1], rawq, wq_hi, 1, wq_split)
            nc.gpsimd.memset(mask[:, :, :], 0.0).then_inc(mask_zero, 1)
            pool.wait_ge(mask_zero, 1)
            nc.gpsimd.affine_select(out=mask[:, :, :], in_=mask[:, :, :], compare_op=ALU.is_ge, fill=MASKED, base=0,
                                    pattern=[[0, GH], [-1, P]], channel_multiplier=1).then_inc(mask_set, 1)
            pool.wait_ge(ident_set, 1)
            nc.gpsimd.tensor_copy(identb[:, :], identf[:, :]).then_inc(identb_set, 1)
            nc.gpsimd.memset(vx[:, :, :, 3 * HD:VW], 1.0).then_inc(ones_set, 1)
            pool.wait_ge(in_o, 32)
            split(wo[:, 0], wo[:, 1], rawo, wo_hi, 1, wo_split)
            split(wr[:, 0], wr[:, 1], wrr[:, :, :], wr_hi, 1, wr_split)
            for pair in range(NB // 2):
                pool.wait_ge(job_lo, job("v", pair))
                r = vres[:, pair % 2, :].rearrange("p (g d) -> p g d", d=HD)
                v = vx[:, 2 * pair:2 * pair + 2, :, :].rearrange("p b h w -> p (b h) w")
                nc.gpsimd.tensor_copy(v[:, :, HD:2 * HD], r).then_inc(v2_done, 1)
                pool.wait_ge(v2_done, pair + 1)
                nc.gpsimd.tensor_tensor(v[:, :, 2 * HD:3 * HD], r, v[:, :, HD:2 * HD],
                                        ALU.subtract).then_inc(v3_done, 1)
            nc.gpsimd.memset(tri[:, :, :], 0.0).then_inc(tri_set, 1)
            pool.wait_ge(tri_set, 1)
            nc.gpsimd.affine_select(out=tri[:, :, :].rearrange("p (t i) j -> p t i j", t=NB),
                                    in_=tri[:, :, :].rearrange("p (t i) j -> p t i j", t=NB), compare_op=ALU.is_ge,
                                    fill=1.0, base=0, pattern=[[0, NB], [-1, E], [1, E]],
                                    channel_multiplier=0).then_inc(tri_set, 1)

            def split_piece(e, n, slot, count):
                part = slice(PIECE * n, PIECE * n + PIECE)
                src = stage[:, slot, part]
                hi = W[:, bass.ds(e, 1), 0, part].rearrange("p e w -> p (e w)")
                lo = W[:, bass.ds(e, 1), 1, part].rearrange("p e w -> p (e w)")
                nc.gpsimd.tensor_tensor(hi, src, one[:, :].to_broadcast([P, PIECE]), ALU.mult).then_inc(w_hi, 1)
                pool.wait_ge(w_hi, count)
                nc.gpsimd.tensor_tensor(lo, src, f(hi), ALU.subtract).then_inc(w_split, 1)

            def body(i, slots):
                for s in slots:
                    if s < PIECES and not (isinstance(i, int) and i >= EARLY):
                        if s == 0:
                            pool.wait_ge(in_w[0], 32 * (i + 1))
                        split_piece(i, s, 0, PIECES * i + s + 1)
                    if due(i, s, POW_LAG, GPB):
                        n = (s - POW_LAG) // GPB
                        u = n % 2
                        pool.wait_ge(eps2, 2 * i + n + 1)
                        nc.gpsimd.tensor_tensor(rstd2[:, u, :], mv2[:, u, 1:2], mhalf[:, 0, :],
                                                ALU.pow).then_inc(rstd2_done, 1)
            schedule(pool, body, NB // 2, TAIL)
            for e in range(EARLY, E):
                slot = (e - EARLY) % 2
                pool.wait_ge(in_w[slot], 32 * ((e - EARLY) // 2 + 1 + (EARLY if slot == 0 else 0)))
                for n in range(PIECES):
                    split_piece(e, n, slot, PIECES * e + n + 1)

        @block.scalar
        def _(act):
            act.wait_ge(in_c, 32)
            nc.scalar.copy(cT[:, 0, :], rawc).then_inc(c_hi, 1)
            for n, (kind, a, hf) in enumerate(JOBS):
                bank = ps[:, n % 8, :]
                act.wait_ge(job_done, n + 1)
                if kind == "k":
                    op = nc.scalar.copy(kT[:, a, bass.ts(hf, HALF)], bank)
                elif kind == "q":
                    op = nc.scalar.activation(qT[:, a, bass.ts(hf, HALF)], bank, ACT.Copy, scale=QSCALE)
                elif kind == "t":
                    op = nc.scalar.copy(xT[:, 0, :, bass.ts(a, 2 * P)], bank.rearrange("p (c t) -> p c t", c=KC))
                else:
                    v = vx[:, 2 * a:2 * a + 2, :, :].rearrange("p b h w -> p (b h) w")
                    op = nc.scalar.copy(v[:, :, 0:HD], bank.rearrange("p (g d) -> p g d", d=HD))
                op.then_inc(job_hi, 1)
            act.wait_ge(in_g, 32)
            nc.scalar.activation(tg[:, :], gate[:, :], ACT.Tanh).then_inc(tg_set, 1)

            def body(i, slots):
                for s in slots:
                    if due(i, s, EVICT_LAG):
                        n = s - EVICT_LAG
                        act.wait_ge(turned, SLOTS * i + n + 1)
                        if not isinstance(i, int) or SLOTS * i + n >= 2:
                            act.wait_ge(pv_done, SLOTS * i + n - 1)
                        nc.scalar.activation(pth[:, n % 2, :], ps[:, 2 + n % 2, :], ACT.Copy,
                                             scale=PSCALE).then_inc(pth_done, 1)
                    if due(i, s, 0):
                        act.wait_ge(negm_done, SLOTS * i + s + 1)
                        if not isinstance(i, int) or i > 0 or s >= 2:
                            act.wait_ge(turned, SLOTS * i + s - 1)
                        else:
                            act.wait_ge(v3_done, NB // 2)
                        for j in range(GH):
                            op = nc.scalar.activation(prob[:, s % 2, j * P:(j + 1) * P],
                                                      ps[:, s % 2, j * P:(j + 1) * P], ACT.Exp,
                                                      bias=negm[:, s % 2, j:j + 1])
                        op.then_inc(exp_done, 1)
                    if due(i, s, ATT_LO_LAG, GPB):
                        n = (s - ATT_LO_LAG) // GPB
                        act.wait_ge(attT_done, 2 * i + n + 1)
                        if not isinstance(i, int) or 2 * i + n >= 1:
                            act.wait_ge(oproj_done, 2 * i + n)
                        nc.scalar.copy(rT[:, 0, 0], ps[:, 6, 0:KC * P].rearrange("p (c t) -> p c t", c=KC)
                                       ).then_inc(attT_hi, 1)
                    if due(i, s, X2T_OUT_LAG, GPB):
                        n = (s - X2T_OUT_LAG) // GPB
                        act.wait_ge(x2T_done, 2 * i + n + 1)
                        nc.scalar.copy(xT[:, 0, :, bass.ts(2 * i + n, P)],
                                       ps[:, 6, 0:KC * P].rearrange("p (c t) -> p c t", c=KC)).then_inc(x2T_hi, 1)
            schedule(act, body, NB // 2, TAIL)

            for hf in range(2):
                act.wait_ge(rt_done, hf + 1)
                nc.scalar.copy(lgT[:, bass.ts(hf, HALF)], ps[0:E, hf, :]).then_inc(rt_out, 1)
            act.wait_ge(rt_exp_in, 1)
            nc.scalar.activation(pr[:, :, :], lg[:, :, :], ACT.Exp).then_inc(rt_exp, 1)

            def moe(i, slots):
                for s in slots:
                    if due(i, s, 0, 1, E * NB):
                        act.wait_ge(gu_done, NB * i + s + 1)
                        if not isinstance(i, int) or i > 0 or s >= 2:
                            act.wait_ge(h_done, NB * i + s - 1)
                        nc.scalar.activation(sg[:, s % 2, 0:D], ps[:, s % 4, 0:D], ACT.Silu).then_inc(silu_done, 1)
                    if due(i, s, 1, 1, E * NB):
                        n = s - 1
                        act.wait_ge(hT_done, NB * i + n + 1)
                        if not isinstance(i, int) or NB * i + n >= 2:
                            act.wait_ge(y_done, NB * i + n - 1)
                        nc.scalar.copy(rT[:, n % 2, 0], ps[:, 4 + n % 2, 0:D].rearrange("p (c t) -> p c t", c=KC)
                                       ).then_inc(hT_hi, 1)
            schedule(act, moe, E, 2)

        @block.vector
        def _(dve):
            nc.vector.memset(f(kbd[:, 0, :, :, :]), 0.0).then_inc(kbd_zeroed, 1)
            for b in range(NB):
                if b % (NB // 2) == 0:
                    dve.wait_ge(in_x[b // (NB // 2)], 16)
                nc.vector.bn_stats(stat[:, b, :], xs[:, b, :]).then_inc(stats1, 1)
            dve.wait_ge(wkv_hi, 1)
            nc.vector.tensor_tensor(wkv[L:P, :], rawkv[L:P, :], f(wkv[L:P, :]), ALU.subtract).then_inc(wkv_split, 1)
            for b in range(NB):
                dve.wait_ge(stats1, b + 1)
                nc.vector.bn_aggr(mv[:, b, :], stat[:, b, :]).then_inc(aggr1, 1)
            dve.wait_ge(aggr1, NB)
            nc.vector.tensor_scalar(mv[:, :, 1:2], mv[:, :, 1:2], EPS, None, ALU.add).then_inc(eps1, 1)

            def job_low(n):
                kind, a, hf = JOBS[n]
                bank = ps[:, n % 8, :]
                dve.wait_ge(job_hi, n + 1)
                if kind == "k":
                    half = bass.ts(hf, HALF)
                    op = nc.vector.tensor_tensor(kT[:, KC + a, half], bank, f(kT[:, a, half]), ALU.subtract)
                elif kind == "q":
                    half = bass.ts(hf, HALF)
                    op = nc.vector.scalar_tensor_tensor(qT[:, KC + a, half], bank, QSCALE, f(qT[:, a, half]),
                                                        ALU.mult, ALU.subtract)
                elif kind == "t":
                    op = nc.vector.tensor_tensor(xT[:, 1, :, bass.ts(a, 2 * P)], bank.rearrange("p (c t) -> p c t", c=KC),
                                                 f(xT[:, 0, :, bass.ts(a, 2 * P)]), ALU.subtract)
                else:
                    if a >= 2:
                        dve.wait_ge(v3_done, a - 1)
                    v = vx[:, 2 * a:2 * a + 2, :, :].rearrange("p b h w -> p (b h) w")
                    op = nc.vector.tensor_tensor(vres[:, a % 2, :].rearrange("p (g d) -> p g d", d=HD),
                                                 bank.rearrange("p (g d) -> p g d", d=HD), v[:, :, 0:HD], ALU.subtract)
                op.then_inc(job_lo, 1)

            for n in range(KC):
                job_low(n)
            dve.wait_ge(rstd1, 1)
            for n in range(KC, len(JOBS)):
                kind, pair, _ = JOBS[n]
                if kind == "t" and pair % 2 == 0:
                    for b in range(2 * pair, 2 * pair + 4):
                        if b >= 4:
                            dve.wait_ge(job_done, job("t", b // 2 - 2))
                        nc.vector.tensor_scalar(nrm[:, b % 4, :], xs[:, b, :], mv[:, b, 0:1], rstd[:, b, :],
                                                ALU.subtract, ALU.mult).then_inc(norm1, 1)
                job_low(n)

            def body(i, slots):
                for s in slots:
                    if due(i, s, 0):
                        dve.wait_ge(scores_done, SLOTS * i + s + 1)
                        if not isinstance(i, int) or i > 0 or s >= 2:
                            dve.wait_ge(exp_done, SLOTS * i + s - 1)
                        nc.vector.tensor_reduce(negm[:, s % 2, :], ps[:, s % 2, :].rearrange("p (h k) -> p h k", h=GH),
                                                AX_X, ALU.max, negate=True).then_inc(negm_done, 1)
                    if due(i, s, EVICT_LAG):
                        n = s - EVICT_LAG
                        dve.wait_ge(pth_done, SLOTS * i + n + 1)
                        if not isinstance(i, int) or SLOTS * i + n >= 2:
                            dve.wait_ge(pv_done, SLOTS * i + n - 1)
                        nc.vector.scalar_tensor_tensor(ptl[:, n % 2, :], ps[:, 2 + n % 2, :], PSCALE,
                                                       pth[:, n % 2, :], ALU.mult, ALU.subtract).then_inc(ptl_done, 1)
                    for part, lag in ((0, HALF0_LAG), (1, HALF1_LAG)):
                        if due(i, s, lag, GPB):
                            n = (s - lag) // GPB
                            half = 2 * (2 * i + n) + part
                            bank = ps[:, 4 + part, :].rearrange("p (h w) -> p h w", w=64)
                            o = slice(P * part, P * part + P)
                            dve.wait_ge(pv_done, GPB * (2 * i + n) + 2 * part + 2)
                            nc.vector.tensor_reduce(attr[:, o].rearrange("p (h d) -> p h d", d=HD),
                                                    bank[:, :, 0:3 * HD].rearrange("p h (c d) -> p h d c", c=3),
                                                    AX_X, ALU.add).then_inc(sums_done, 1)
                            nc.vector.reciprocal(rinv[:, :].unsqueeze(2),
                                                 bank[:, :, 3 * HD:3 * HD + 1]).then_inc(sums_done, 1)
                            dve.wait_ge(sums_done, 2 * half + 2)
                            if not isinstance(i, int) or 2 * i + n >= 1:
                                dve.wait_ge(attT_done, 2 * i + n)
                            nc.vector.tensor_tensor(att[:, o].rearrange("p (h d) -> p h d", d=HD),
                                                    attr[:, o].rearrange("p (h d) -> p h d", d=HD),
                                                    rinv[:, :].unsqueeze(2).to_broadcast([P, HPC, HD]),
                                                    ALU.mult).then_inc(att_done, 1)
                    if due(i, s, NORM2_LAG, GPB):
                        n = (s - NORM2_LAG) // GPB
                        b, u = 2 * i + n, n % 2
                        dve.wait_ge(rstd2_done, b + 1)
                        if not isinstance(i, int) or b >= 2:
                            dve.wait_ge(x2T_done, b)
                        nc.vector.tensor_scalar(nrm[:, u, :], nrm[:, 2 + u, :], rstd2[:, u, :], None,
                                                ALU.mult).then_inc(norm2, 1)
                    if due(i, s, ATT_LO_LAG, GPB):
                        n = (s - ATT_LO_LAG) // GPB
                        dve.wait_ge(attT_hi, 2 * i + n + 1)
                        if not isinstance(i, int) or 2 * i + n >= 1:
                            dve.wait_ge(oproj_done, 2 * i + n)
                        nc.vector.tensor_tensor(rT[:, 0, 1], ps[:, 6, 0:KC * P].rearrange("p (c t) -> p c t", c=KC),
                                                f(rT[:, 0, 0]), ALU.subtract).then_inc(attT_lo, 1)
                    if due(i, s, X1_LAG, GPB):
                        n = (s - X1_LAG) // GPB
                        b, u = 2 * i + n, n % 2
                        xb = xs[:, bass.ds(b, 1), :].rearrange("p b d -> p (b d)")
                        dve.wait_ge(oproj_done, b + 1)
                        if isinstance(i, int) and 2 * i + n == 0:
                            dve.wait_ge(tg_set, 1)
                        nc.vector.scalar_tensor_tensor(xb, ps[:, 7, 0:D], tg[:, 0:1], xb, ALU.mult, ALU.add,
                                                       accum_out=mv2[:, u, 0:1]).then_inc(x1_done, 1)
                        dve.wait_ge(x1_done, b + 1)
                        nc.vector.tensor_scalar(mv2[:, u, 0:1], mv2[:, u, 0:1], 1.0 / D, None,
                                                ALU.mult).then_inc(mean2, 1)
                        dve.wait_ge(mean2, b + 1)
                        nc.vector.tensor_scalar(nrm[:, 2 + u, :], xb, mv2[:, u, 0:1], None,
                                                ALU.subtract).then_inc(centred2, 1)
                        dve.wait_ge(centred2, b + 1)
                        nc.vector.tensor_tensor_reduce(junk[:, :], nrm[:, 2 + u, :], nrm[:, 2 + u, :], 1.0, 0.0,
                                                       ALU.mult, ALU.add, mv2[:, u, 1:2]).then_inc(squares2, 1)
                        dve.wait_ge(squares2, b + 1)
                        nc.vector.tensor_scalar(mv2[:, u, 1:2], mv2[:, u, 1:2], 1.0 / D, EPS,
                                                ALU.mult, ALU.add).then_inc(eps2, 1)
                    if due(i, s, X2T_OUT_LAG, GPB):
                        n = (s - X2T_OUT_LAG) // GPB
                        b = 2 * i + n
                        dve.wait_ge(x2T_hi, b + 1)
                        nc.vector.tensor_tensor(xT[:, 1, :, bass.ts(b, P)],
                                                ps[:, 6, 0:KC * P].rearrange("p (c t) -> p c t", c=KC),
                                                f(xT[:, 0, :, bass.ts(b, P)]), ALU.subtract).then_inc(x2T_lo, 1)
            schedule(dve, body, NB // 2, TAIL)

            steps = [0]

            def step(ins):
                steps[0] += 1
                ins.then_inc(rt_step, 1)
                dve.wait_ge(rt_step, steps[0])

            def over_e(ap):
                return ap.unsqueeze(2).to_broadcast([P, NB, E])

            dve.wait_ge(rt_T, 1)
            step(nc.vector.tensor_copy(lg[:, :, :], ps[:, 2, 0:NB * E].rearrange("p (t e) -> p t e", e=E)))
            step(nc.vector.tensor_reduce(lmax[:, :], lg[:, :, :], AX_X, ALU.max))
            nc.vector.tensor_tensor(lg[:, :, :], lg[:, :, :], over_e(lmax[:, :]), ALU.subtract).then_inc(rt_exp_in, 1)
            dve.wait_ge(rt_exp, 1)
            step(nc.vector.tensor_reduce(psum_r[:, :], pr[:, :, :], AX_X, ALU.add))
            step(nc.vector.reciprocal(psum_r[:, :], psum_r[:, :]))
            step(nc.vector.tensor_tensor(pr[:, :, :], pr[:, :, :], over_e(psum_r[:, :]), ALU.mult))
            pj = pr[:, :, :].unsqueeze(2).to_broadcast([P, NB, E, E])
            pi = pr[:, :, :].unsqueeze(3).to_broadcast([P, NB, E, E])
            step(nc.vector.tensor_tensor(cmpa, pj, pi, ALU.is_gt))
            step(nc.vector.tensor_tensor(cmpb, pj, pi, ALU.is_equal))
            dve.wait_ge(tri_set, 2)
            tri_v = tri[:, :, :].rearrange("p (t i) j -> p t i j", t=NB)
            step(nc.vector.tensor_tensor(cmpb, cmpb, tri_v, ALU.mult))
            step(nc.vector.tensor_tensor(cmpa, cmpa, cmpb, ALU.add))
            step(nc.vector.tensor_reduce(rank[:, :, :], cmpa, AX_X, ALU.add))
            step(nc.vector.scalar_tensor_tensor(pr[:, :, :], rank[:, :, :], 2.0, pr[:, :, :], ALU.is_lt, ALU.mult))
            step(nc.vector.tensor_reduce(psum_r[:, :], pr[:, :, :], AX_X, ALU.add))
            step(nc.vector.reciprocal(psum_r[:, :], psum_r[:, :]))
            step(nc.vector.tensor_scalar(psum_r[:, :], psum_r[:, :], tg[:, 1:2], None, ALU.mult))
            nc.vector.tensor_tensor(wtok[:, :, :].rearrange("p e t -> p t e"), pr[:, :, :], over_e(psum_r[:, :]),
                                    ALU.mult).then_inc(w_ready, 1)

            def moe(i, slots):
                for s in slots:
                    if due(i, s, 0, 1, E * NB):
                        dve.wait_ge(silu_done, NB * i + s + 1)
                        if not isinstance(i, int) or i > 0 or s >= 2:
                            dve.wait_ge(hT_done, NB * i + s - 1)
                        nc.vector.tensor_tensor(h[:, s % 2, :], ps[:, s % 4, D:2 * D], sg[:, s % 2, 0:D],
                                                ALU.mult).then_inc(h_done, 1)
                    if due(i, s, 1, 1, E * NB):
                        n = s - 1
                        dve.wait_ge(hT_hi, NB * i + n + 1)
                        if not isinstance(i, int) or NB * i + n >= 2:
                            dve.wait_ge(y_done, NB * i + n - 1)
                        nc.vector.tensor_tensor(rT[:, n % 2, 1],
                                                ps[:, 4 + n % 2, 0:D].rearrange("p (c t) -> p c t", c=KC),
                                                f(rT[:, n % 2, 0]), ALU.subtract).then_inc(hT_lo, 1)
                    if due(i, s, 3, 1, E * NB):
                        n = s - 3
                        t = n % NB
                        e = i + n // NB
                        dve.wait_ge(y_done, NB * i + n + 1)
                        if isinstance(i, int) and i == 0 and n == 0:
                            dve.wait_ge(w_ready, 1)
                        if not isinstance(i, int) or e > 0:
                            dve.wait_ge(acc_done, NB * i + n)
                        wt = wtok[:, bass.ds(e, 1), t]
                        nc.vector.scalar_tensor_tensor(xs[:, t, :], ps[:, 6 + n % 2, 0:D], wt, xs[:, t, :],
                                                       ALU.mult, ALU.add).then_inc(acc_done, 1)
            schedule(dve, moe, E, 3)

        @block.tensor
        def _(pe):
            def mm3(out_, a_hi, a_lo, b_hi, b_lo, first, last):
                nc.tensor.matmul(out_, a_hi, b_hi, start=first, stop=False)
                nc.tensor.matmul(out_, a_hi, b_lo, start=False, stop=False)
                return nc.tensor.matmul(out_, a_lo, b_hi, start=False, stop=last)

            for n, (kind, a, hf) in enumerate(JOBS):
                bank = ps[:, n % 8, :]
                half = bass.ts(hf, HALF)
                if n == 0:
                    pe.wait_ge(wkv_split, 1)
                    pe.wait_ge(c_split, 1)
                if n >= 8:
                    pe.wait_ge(job_lo, n - 7)
                if kind == "k":
                    w = wkv[:, a * P:(a + 1) * P]
                    nc.tensor.matmul(bank, w, cT[:, 0, half], start=True, stop=False)
                    mm = nc.tensor.matmul(bank, w, cT[:, 1, half], start=False, stop=True)
                elif kind == "v":
                    for u in range(2):
                        o = bank[:, D * u:D * u + D]
                        tok = bass.ts(2 * a + u, P)
                        nc.tensor.matmul(o, cT[:, 0, tok], wkv[:, D:2 * D], start=True, stop=False)
                        mm = nc.tensor.matmul(o, cT[:, 1, tok], wkv[:, D:2 * D], start=False, stop=True)
                elif kind == "t":
                    pe.wait_ge(ident_set, 1)
                    pe.wait_ge(norm1, 2 * a + 2)
                    for u in range(2):
                        for c in range(KC):
                            mm = nc.tensor.transpose(bank[:, 2 * P * c + P * u:2 * P * c + P * u + P],
                                                     nrm[:, (2 * a + u) % 4, c * P:(c + 1) * P], identf[:, :])
                else:
                    pe.wait_ge(wq_split, 1)
                    pe.wait_ge(job_lo, job("t", 2 * hf + 1))
                    for c in range(KC):
                        m = slice(a * P, (a + 1) * P)
                        mm = mm3(bank, wq[:, 0, c, m], wq[:, 1, c, m], xT[:, 0, c, half], xT[:, 1, c, half],
                                 c == 0, c == KC - 1)
                mm.then_inc(job_done, 1)

            pe.wait_ge(job_lo, len(JOBS))
            pe.wait_ge(mask_set, 1)
            pe.wait_ge(identb_set, 1)
            pe.wait_ge(ones_set, 1)
            pe.wait_ge(v3_done, NB // 2)
            pe.wait_ge(wo_split, 1)

            def body(i, slots):
                for s in slots:
                    if due(i, s, 0):
                        u, g = s // GPB, s % GPB
                        c, j0 = g // 2, GH * (g % 2)
                        if g == 0:
                            pe.wait_ge(kq_loaded[u], PREFETCHES * (i + 1))
                        if not isinstance(i, int) or i > 0 or s >= 2:
                            pe.wait_ge(exp_done, SLOTS * i + s - 1)
                        bank = ps[:, s % 2, :]

                        def keys(part):
                            return kbd[:, u, KC * part + c, j0:j0 + GH, :].rearrange("p h k -> p (h k)")
                        nc.tensor.matmul(bank, identb[:, :], mask[:, :, :].rearrange("p h k -> p (h k)"),
                                         start=True, stop=False)
                        mm3(bank, qb[:, u, c, :], qb[:, u, KC + c, :], keys(0), keys(1), False, True
                            ).then_inc(scores_done, 1)
                    if due(i, s, TURN_LAG):
                        n = s - TURN_LAG
                        pe.wait_ge(exp_done, SLOTS * i + n + 1)
                        if not isinstance(i, int) or SLOTS * i + n >= 2:
                            pe.wait_ge(ptl_done, SLOTS * i + n - 1)
                        for j in range(GH):
                            mm = nc.tensor.transpose(ps[:, 2 + n % 2, j * P:(j + 1) * P],
                                                     prob[:, n % 2, j * P:(j + 1) * P], identf[:, :])
                        mm.then_inc(turned, 1)
                    if due(i, s, PV_LAG):
                        n = s - PV_LAG
                        g = n % GPB
                        b = 2 * i + n // GPB
                        pe.wait_ge(ptl_done, SLOTS * i + n + 1)
                        if g % 2 == 0 and (not isinstance(i, int) or 2 * i + n // GPB >= 1):
                            pe.wait_ge(sums_done, 4 * (b - 1) + g + 2)
                        for j in range(GH):
                            hh = GH * (g % 2) + j
                            o = ps[:, 4 + g // 2, 64 * hh:64 * hh + 3 * HD + 1]
                            v = vx[:, bass.ds(b, 1), GH * g + j, 0:3 * HD + 1].rearrange("p b w -> p (b w)")
                            nc.tensor.matmul(o, pth[:, n % 2, j * P:(j + 1) * P], v, start=True, stop=False)
                            mm = nc.tensor.matmul(o, ptl[:, n % 2, j * P:(j + 1) * P], v, start=False, stop=True)
                        mm.then_inc(pv_done, 1)
                    if due(i, s, ATT_T_LAG, GPB):
                        n = (s - ATT_T_LAG) // GPB
                        b = 2 * i + n
                        pe.wait_ge(att_done, 2 * b + 2)
                        if not isinstance(i, int) or b >= 1:
                            pe.wait_ge(x2T_lo, b)
                        for c in range(KC):
                            mm = nc.tensor.transpose(ps[:, 6, c * P:(c + 1) * P], att[:, c * P:(c + 1) * P], identf[:, :])
                        mm.then_inc(attT_done, 1)
                    if due(i, s, OPROJ_LAG, GPB):
                        n = (s - OPROJ_LAG) // GPB
                        b = 2 * i + n
                        pe.wait_ge(attT_lo, b + 1)
                        if not isinstance(i, int) or b >= 1:
                            pe.wait_ge(x1_done, b)
                        for c in range(KC):
                            mm = mm3(ps[:, 7, 0:D], rT[:, 0, 0, c, :], rT[:, 0, 1, c, :], wo[:, 0, c, :], wo[:, 1, c, :],
                                     c == 0, c == KC - 1)
                        mm.then_inc(oproj_done, 1)
                    if due(i, s, X2T_LAG, GPB):
                        n = (s - X2T_LAG) // GPB
                        b, u = 2 * i + n, n % 2
                        pe.wait_ge(norm2, b + 1)
                        pe.wait_ge(attT_lo, b + 1)
                        for c in range(KC):
                            mm = nc.tensor.transpose(ps[:, 6, c * P:(c + 1) * P], nrm[:, u, c * P:(c + 1) * P],
                                                     identf[:, :])
                        mm.then_inc(x2T_done, 1)
            schedule(pe, body, NB // 2, TAIL)

            pe.wait_ge(x2T_lo, NB)
            pe.wait_ge(wr_split, 1)
            for hf in range(2):
                half = bass.ts(hf, HALF)
                for c in range(KC):
                    mm = mm3(ps[0:E, hf, :], wr[:, 0, c, :], wr[:, 1, c, :], xT[:, 0, c, half], xT[:, 1, c, half],
                             c == 0, c == KC - 1)
                mm.then_inc(rt_done, 1)
            pe.wait_ge(rt_out, 2)
            for t in range(NB):
                mm = nc.tensor.transpose(ps[:, 2, E * t:E * t + E], lgT[:, t * P:(t + 1) * P], identf[0:E, 0:E])
            mm.then_inc(rt_T, 1)

            def moe(i, slots):
                for s in slots:
                    if due(i, s, 0, 1, E * NB):
                        if s == 0:
                            pe.wait_ge(w_split, PIECES * (i + 1))
                        if isinstance(i, int) and i == 0:
                            if s == 2:
                                pe.wait_ge(rt_step, 1)
                            if s >= 4:
                                pe.wait_ge(h_done, s - 3)
                        else:
                            pe.wait_ge(h_done, NB * i + s - 3)
                        for c in range(KC):
                            def w(part):
                                return W[:, bass.ds(i, 1), part, c * F2:(c + 1) * F2].rearrange("p e w -> p (e w)")
                            x_hi, x_lo = xT[:, 0, c, s * P:(s + 1) * P], xT[:, 1, c, s * P:(s + 1) * P]
                            mm = mm3(ps[:, s % 4, :], x_hi, x_lo, w(0), w(1), c == 0, c == KC - 1)
                        mm.then_inc(gu_done, 1)
                    if due(i, s, 1, 1, E * NB):
                        n = s - 1
                        pe.wait_ge(h_done, NB * i + n + 1)
                        if not isinstance(i, int) or NB * i + n >= 2:
                            pe.wait_ge(hT_lo, NB * i + n - 1)
                        for c in range(KC):
                            mm = nc.tensor.transpose(ps[:, 4 + n % 2, c * P:(c + 1) * P],
                                                     h[:, n % 2, c * P:(c + 1) * P], identf[:, :])
                        mm.then_inc(hT_done, 1)
                    if due(i, s, 2, 1, E * NB):
                        n = s - 2
                        e = i + n // NB
                        pe.wait_ge(hT_lo, NB * i + n + 1)
                        if not isinstance(i, int) or NB * i + n >= 2:
                            pe.wait_ge(acc_done, NB * i + n - 1)
                        for c in range(KC):
                            def w(part):
                                at = KC * F2 + c * D
                                return W[:, bass.ds(e, 1), part, at:at + D].rearrange("p e w -> p (e w)")
                            mm = mm3(ps[:, 6 + n % 2, 0:D], rT[:, n % 2, 0, c, :], rT[:, n % 2, 1, c, :], w(0), w(1),
                                     c == 0, c == KC - 1)
                        mm.then_inc(y_done, 1)
            schedule(pe, moe, E, 2)


def kernel(x, ctx_512, g_xattn, g_ffn, L0_xattn_Wq, L0_xattn_Wkv_expand, L0_xattn_Wout, L0_ffn_Wr, L0_ffn_Wg,
           L0_ffn_Wu, L0_ffn_Wd):
    import numpy as np
    import concourse.bacc as bacc
    from concourse import mybir
    from concourse.bass_utils import run_bass_kernel_spmd

    B, S, D = x.shape
    arrays = {
        "x": np.asarray(x).reshape(B * S, D),
        "ctxT": np.asarray(ctx_512).reshape(B * S, -1).T,
        "g_attn": np.asarray(g_xattn),
        "g_ffn": np.asarray(g_ffn),
        "WqT": np.asarray(L0_xattn_Wq).T,
        "WkvT": np.asarray(L0_xattn_Wkv_expand).T,
        "WoT": np.asarray(L0_xattn_Wout).T,
        "Wr": np.asarray(L0_ffn_Wr),
        "Wgu": np.concatenate([np.asarray(L0_ffn_Wg), np.asarray(L0_ffn_Wu)], axis=2),
        "Wd": np.asarray(L0_ffn_Wd),
    }
    arrays = {n: np.ascontiguousarray(a) for n, a in arrays.items()}
    nc = bacc.Bacc("TRN2", target_bir_lowering=False, num_devices=1)
    args = [nc.dram_tensor(n, a.shape, mybir.dt.from_np(a.dtype), kind="ExternalInput").ap() for n, a in arrays.items()]
    out = nc.dram_tensor("out", (B * S, D), mybir.dt.float32, kind="ExternalOutput").ap()
    build_gated_block(nc, *args, out)
    r = run_bass_kernel_spmd(nc, [arrays], core_ids=[0])
    return r.results[0]["out"].reshape(B, S, D)
```

```python
from contextlib import ExitStack

import concourse.bass as bass
from concourse import mybir

ALU = mybir.AluOpType
ACT = mybir.ActivationFunctionType
AX_X = mybir.AxisListType.X
F32 = mybir.dt.float32
F32R = mybir.dt.float32r
BF16 = mybir.dt.bfloat16
F16 = mybir.dt.float16
U32 = mybir.dt.uint32

P = 128
MASKED = -3.0e38


def build_gated_block(nc, x, ctxT, g_attn, g_ffn, WqT, WkvT, WoT, Wr, Wgu, Wd, consts, consts16, out):
    NTOK, D = x.shape
    L = ctxT.shape[0]
    NB = NTOK // P
    KC = D // P
    HD = 16
    NH = D // HD
    HPC = P // HD
    E, _, F2 = Wgu.shape
    GH = 4
    GPB = NH // GH
    NG = NB * GPB
    SLOTS = 2 * GPB
    VW = 3 * HD + 2
    BANK = 512
    WPE = KC * F2 + KC * D
    PIECE = 512
    PIECES = WPE // PIECE
    TOPK = 2
    NTILES = TOPK * NB + E - 1
    ROUNDS = (NTILES + 1) // SLOTS
    QSCALE = HD ** -0.5
    PSCALE = 4096.0
    EPS = 1e-5
    ROUND = 1.5 * 2.0 ** 23
    assert L * 2 == P and D == KC * P and F2 == 2 * D and NB == 8 and E == 8 and (NTILES + 1) % SLOTS == 0

    with ExitStack() as ctx:
        def sb(name, shape, dt=F32):
            return ctx.enter_context(nc.sbuf_tensor(name, shape, dt))

        def sem(name):
            return ctx.enter_context(nc.semaphore(name))

        ps = ctx.enter_context(nc.psum_tensor("ps", [P, 8, BANK], F32))

        xs = sb("xs", [P, NB, D])
        nrm = sb("nrm", [P, 4, D])
        xT = sb("xT", [P, 2, KC, NTOK], F32R)
        kbd = sb("kbd", [P, 2, 4, HPC, P], F32R)
        qb = sb("qb", [P, 2, 4, P], F32R)
        vx = sb("vx", [P, NB, NH, VW], BF16)
        W = sb("W", [P, E, 2, WPE], F32R)
        stage = sb("stage", [P, 2, WPE])
        prob = sb("prob", [P, 2, BANK])
        pth = sb("pth", [P, 2, BANK], F16)
        ptl = sb("ptl", [P, 2, BANK], F16)
        attr = sb("attr", [P, D])
        att = sb("att", [P, D])
        rT = sb("rT", [P, 2, 2, KC, P], F32R)
        wo = sb("wo", [P, 2, KC, D], F32R)
        wrr = sb("wrr", [P, KC, E])
        wr = sb("wr", [P, 2, KC, E], F32R)
        cst = sb("cst", list(consts.shape))
        cst16 = sb("cst16", list(consts16.shape), BF16)
        stat = sb("stat", [P, NB, 6])
        mv = sb("mv", [P, NB, 2])
        rstd = sb("rstd", [P, NB, 1])
        junk = sb("junk", [P, D], BF16)
        mv2 = sb("mv2", [P, 2, 2])
        rstd2 = sb("rstd2", [P, 2, 1])
        mhalf = sb("mhalf", [P, NB, 1])
        one = sb("one", [P, 1])
        negm = sb("negm", [P, 2, GH])
        rinv = sb("rinv", [P, HPC])
        gate = sb("gate", [P, 2])
        tg = sb("tg", [P, 2])
        lg = sb("lg", [P, NB, E])
        lmax = sb("lmax", [P, NB])
        pr = sb("pr", [P, NB, E])
        psum_r = sb("psum_r", [P, NB])
        rank = sb("rank", [P, NB, E])
        chosen = sb("chosen", [P, NB, E], BF16)
        J = NTILES + 1
        tile_expert = sb("tile_expert", [P, J], U32)
        idx = sb("idx", [P, 2, J], U32)
        xnd = nc.dram_tensor("xnd", (NTOK, D), F32, kind="Internal").ap()
        yout = nc.dram_tensor("yout", (TOPK * NTOK + NTILES * P, D), F32, kind="Internal").ap()

        cuts = [0]

        def const(n):
            cuts[0] += n
            return cst[:, cuts[0] - n:cuts[0]]
        identf = const(P)
        fulls = const(NB).unsqueeze(1).to_broadcast([P, E, NB])
        upto = const(E * E).rearrange("p (e j) -> p e j", e=E)
        tri = const(E * E).rearrange("p (i j) -> p i j", i=E)
        tile_no = const(J)
        part_no = const(1)
        block_no = const(TOPK * NB)
        empty_row = const(J)
        mask, identb, before, ones, col_no = (cst16[:, P * k:P * k + P] for k in range(5))

        late = W[:, 5:E, :, :].rearrange("p e h w -> p (e h w)")
        NQ = 4 * NTOK
        qT = late[:, 0:NQ].rearrange("p (a t) -> p a t", a=4)
        kT = late[:, NQ:2 * NQ].rearrange("p (a t) -> p a t", a=4)
        at = 2 * NQ
        wq = late[:, at:at + 2 * KC * D].rearrange("p (a c n) -> p a c n", a=2, c=KC)
        late = W[:, 4, :, :].rearrange("p h w -> p (h w)")
        cT = late[:, 0:2 * NTOK].rearrange("p (a t) -> p a t", a=2)
        at = 2 * NTOK
        wkv = late[:, at:at + 2 * D]
        rawq = stage[:, 0, 0:512].rearrange("p (c n) -> p c n", c=KC)
        rawo = stage[:, 0, 512:1024].rearrange("p (c n) -> p c n", c=KC)
        rawkv = stage[:, 0, 1024:1536]
        rawc = stage[:, 1, 0:NTOK]
        vres = prob
        sg = prob
        h = nrm

        lgT = prob[0:E, :, :].rearrange("p a n -> p (a n)")
        cmp2 = vx[:, 0:NB // 2, :, :].rearrange("p b h w -> p (b h w)")[:, 0:4 * NB * E * E].bitcast(F32)
        cmpa, cmpb = (cmp2[:, NB * E * E * k:NB * E * E * (k + 1)].rearrange("p (t i j) -> p t i j", t=NB, i=E)
                      for k in range(2))
        scr = vx[:, NB // 2:NB, :, :].rearrange("p b h w -> p (b h w)").bitcast(F32)
        scr_cuts = [0]

        def scratch(n):
            scr_cuts[0] += n
            return scr[:, scr_cuts[0] - n:scr_cuts[0]]
        choice = scratch(TOPK * NB * E).rearrange("p (k t e) -> p k t e", k=TOPK, t=NB)
        picked = scratch(TOPK * NB * E).rearrange("p (k t e) -> p k t e", k=TOPK, t=NB)
        wk = scratch(TOPK * NB).rearrange("p (k t) -> p k t", k=TOPK)
        rank_k = scratch(TOPK * NB)
        over = scratch(TOPK * NB)
        nfull = scratch(TOPK * NB)
        place = scratch(TOPK * NB)
        tile_k = scratch(TOPK * NB)
        full = scratch(E * NB).rearrange("p (e k) -> p e k", e=E)
        ntiles = scratch(E)
        cum = scratch(E * E).rearrange("p (e j) -> p e j", e=E)
        cum_end, cum_start = scratch(E), scratch(E)
        past = scratch(J * E).rearrange("p (j e) -> p j e", e=E)
        tile_e, v1, e0, c0 = (scratch(J) for _ in range(4))
        in_tile = scratch(TOPK * NB * J).rearrange("p (m j) -> p m j", j=J)
        vflat = vx[:, 0:NB // 2, :, :].rearrange("p b h w -> p (b h w)")
        NA = TOPK * NB * P
        at_place = vflat[:, 0:NA].rearrange("p (m q) -> p m q", q=P)
        at_tile = vflat[:, NA:NA + TOPK * NB * 2 * J].rearrange("p (m v j) -> p m v j", v=2, j=J)
        kflat = kbd[:, :, :, :, :].rearrange("p u a h k -> p (u a h k)").bitcast(F32)
        xg = kflat[:, 0:SLOTS * D].rearrange("p (s d) -> p s d", d=D)
        yk = kflat[:, SLOTS * D:(SLOTS + TOPK * NB) * D].rearrange("p (k t d) -> p k t d", k=TOPK, d=D)
        ys = stage[:, :, :].rearrange("p s w -> p (s w)")[:, 0:SLOTS * D].rearrange("p (s d) -> p s d", d=D)

        def f(ap):
            return ap.bitcast(F32)

        in_x = [sem(f"in_x{i}") for i in range(2)]
        in_kv, in_c, in_q, in_o, in_g = (sem("in_" + n) for n in ("kv", "c", "q", "o", "g"))
        in_const = sem("in_const")
        ones_set, mhalf_set, kbd_zeroed = sem("ones_set"), sem("mhalf_set"), sem("kbd_zeroed")
        wkv_hi, wkv_split, c_hi, c_split = (sem(n) for n in ("wkv_hi", "wkv_split", "c_hi", "c_split"))
        wq_hi, wq_split, wo_hi, wo_split, wr_hi, wr_split = (
            sem(n) for n in ("wq_hi", "wq_split", "wo_hi", "wo_split", "wr_hi", "wr_split"))
        stats1, aggr1, eps1, rstd1, norm1 = (sem(n) for n in ("stats1", "aggr1", "eps1", "rstd1", "norm1"))
        job_done, job_hi, job_lo, v2_done, v3_done = (
            sem(n) for n in ("job_done", "job_hi", "job_lo", "v2_done", "v3_done"))
        tg_set = sem("tg_set")
        kq_loaded = [sem(f"kq_loaded{u}") for u in range(2)]
        scores_done, negm_done, exp_done, turned, pth_done, ptl_done, pv_done = (
            sem(n) for n in ("scores_done", "negm_done", "exp_done", "turned", "pth_done", "ptl_done", "pv_done"))
        sums_done, att_done, attT_done, attT_hi, attT_lo, oproj_done, x1_done = (
            sem(n) for n in ("sums_done", "att_done", "attT_done", "attT_hi", "attT_lo", "oproj_done", "x1_done"))
        mean2, centred2, squares2, eps2, rstd2_done, norm2, x2T_done, x2T_hi, x2T_lo = (
            sem(n) for n in ("mean2", "centred2", "squares2", "eps2", "rstd2_done", "norm2", "x2T_done", "x2T_hi", "x2T_lo"))
        in_w, w_hi, w_split = [sem("in_w0"), sem("in_w1")], sem("w_hi"), sem("w_split")
        rt_done, rt_out, rt_T, rt_step, rt_exp_in, rt_exp = (
            sem(n) for n in ("rt_done", "rt_out", "rt_T", "rt_step", "rt_exp_in", "rt_exp"))
        xn_stored = [sem(f"xn_stored{u}") for u in range(2)]
        chosen_set, counted, sorted_in, sorted_out, idx_set, experts_set = (
            sem(n) for n in ("chosen_set", "counted", "sorted_in", "sorted_out", "idx_set", "experts_set"))
        xg_in = [sem(f"xg_in{s}") for s in range(SLOTS)]
        y_sent = [sem(f"y_sent{s}") for s in range(SLOTS)]
        xgT_done, xgT_hi, xgT_lo = sem("xgT_done"), sem("xgT_hi"), sem("xgT_lo")
        gu_done, silu_done, h_done, hT_done, hT_hi, hT_lo, y_done, y_out = (
            sem(n) for n in ("gu_done", "silu_done", "h_done", "hT_done", "hT_hi", "hT_lo", "y_done", "y_out"))
        yk_in = [[sem(f"yk_in{k}{q}") for q in range(2)] for k in range(TOPK)]
        add0_done, add1_done = sem("add0_done"), sem("add1_done")
        out_done = sem("out_done")

        x_v = x.rearrange("(b p) d -> p b d", p=P)
        out_v = out.rearrange("(b p) d -> p b d", p=P)
        TURN_LAG, EVICT_LAG, PV_LAG, HALF0_LAG, HALF1_LAG = 1, 2, 3, 5, 7
        ATT_T_LAG, ATT_LO_LAG, OPROJ_LAG, X1_LAG, POW_LAG, NORM2_LAG, X2T_LAG, X2T_OUT_LAG = 8, 8, 9, 9, 9, 10, 11, 11
        TAIL = X2T_OUT_LAG - GPB + 1
        PREFETCHES = 16 * (HPC + 1)

        def due(i, s, lag, step=1, last=NG):
            n = s - lag
            if n % step:
                return False
            return not isinstance(i, int) or 0 <= SLOTS * i + n < last

        def schedule(eng, body, iterations, tail):
            body(0, range(SLOTS))
            with eng.Fori(1, iterations) as i:
                body(i, range(SLOTS))
            body(iterations, range(tail))

        X_LAG, GU_LAG, H_LAG, Y_LAG, SEND_LAG = 0, 1, 2, 3, 7

        def tile_due(i, s, lag):
            return not isinstance(i, int) or 1 <= SLOTS * i + s - lag <= NTILES

        def tile_past(i, s, lag, back):
            return not isinstance(i, int) or SLOTS * i + s - lag > back

        HALF = NTOK // 2
        JOBS = []
        for hf in range(2):
            JOBS += [("k", mc, hf) for mc in range(KC)] + [("t", 2 * hf, 0), ("t", 2 * hf + 1, 0)]
            JOBS += [("q", mc, hf) for mc in range(KC)] + [("v", 2 * hf, 0), ("v", 2 * hf + 1, 0)]
        HALF_JOBS = len(JOBS) // 2

        def job(kind, a, hf=0):
            return JOBS.index((kind, a, hf)) + 1

        block = ctx.enter_context(nc.Block())

        @block.sync
        def _(sp):
            sp.dma_start(xs[:, 0:NB // 2, :], x_v[:, 0:NB // 2, :]).then_inc(in_x[0], 16)
            for half in range(2):
                sp.dma_start(rawkv[L * half:L * half + L, :], WkvT).then_inc(in_kv, 16)
            for half in range(2):
                sp.dma_start(rawc[L * half:L * half + L, :], ctxT).then_inc(in_c, 16)
            sp.dma_start(xs[:, NB // 2:NB, :], x_v[:, NB // 2:NB, :]).then_inc(in_x[1], 16)
            sp.dma_start(cst[:, :], consts).then_inc(in_const, 16)
            sp.dma_start(cst16[:, :], consts16).then_inc(in_const, 16)
            sp.dma_start(rawq, WqT.rearrange("(c p) n -> p c n", p=P)).then_inc(in_q, 16)
            sp.dma_start(gate[:, 0:1], g_attn.partition_broadcast(P)).then_inc(in_g, 16)
            sp.dma_start(gate[:, 1:2], g_ffn.partition_broadcast(P)).then_inc(in_g, 16)
            sp.dma_start(rawo, WoT.rearrange("(c p) n -> p c n", p=P)).then_inc(in_o, 16)
            sp.dma_start(wrr[:, :, :], Wr.rearrange("(c p) n -> p c n", p=P)).then_inc(in_o, 16)
            sp.wait_ge(job_hi, job("q", KC - 1, 0))
            sp.wait_ge(job_lo, job("q", KC - 1, 0))
            sp.wait_ge(kbd_zeroed, 2)

            def prefetch(u, b):
                for j in range(HPC):
                    rows = slice(HD * j, HD * j + HD)
                    sp.dma_start(f(kbd[rows, u, :, j, :]), f(kT[rows, :, bass.ts(b, P)])).then_inc(kq_loaded[u], 16)
                sp.dma_start(f(qb[:, u, :, :]), f(qT[:, :, bass.ts(b, P)])).then_inc(kq_loaded[u], 16)

            def load_expert(e, slot):
                sp.dma_start(stage[:, slot, 0:KC * F2].rearrange("p (c n) -> p c n", c=KC),
                             Wgu[e].rearrange("(c p) n -> p c n", p=P)).then_inc(in_w[slot], 16)
                sp.dma_start(stage[:, slot, KC * F2:].rearrange("p (c n) -> p c n", c=KC),
                             Wd[e].rearrange("(c p) n -> p c n", p=P)).then_inc(in_w[slot], 16)

            prefetch(0, 0)
            prefetch(1, 1)
            sp.wait_ge(wq_split, 1)
            sp.wait_ge(wkv_split, 1)
            sp.wait_ge(wo_split, 1)
            load_expert(0, 1)
            sp.wait_ge(job_lo, len(JOBS))

            def feed(i):
                sp.wait_ge(scores_done, SLOTS * i - GPB)
                prefetch(0, 2 * i)
                if not isinstance(i, int) or i > 1:
                    sp.wait_ge(w_split, 2 * PIECES * (i - 1))
                load_expert(2 * i - 1, 0)
                sp.wait_ge(scores_done, SLOTS * i)
                prefetch(1, 2 * i + 1)
                sp.wait_ge(w_split, PIECES * (2 * i - 1))
                load_expert(2 * i, 1)
            feed(1)
            with sp.Fori(2, NB // 2) as i:
                feed(i)
            sp.wait_ge(w_split, PIECES * (E - 2))
            load_expert(E - 1, 0)

            for s in range(SLOTS):
                sp.wait_ge(y_sent[s], 16 * (ROUNDS if s > 0 else ROUNDS - 1))
            yout_v = yout[0:TOPK * NTOK, :].rearrange("(k b p) d -> k p b d", k=TOPK, p=P)
            for q in range(2):
                part = slice(q * NB // 2, (q + 1) * NB // 2)
                for k in range(TOPK):
                    sp.dma_start(yk[:, k, part, :], yout_v[k, :, part, :]).then_inc(yk_in[k][q], 16)
            for t in range(NB):
                sp.wait_ge(add1_done, t + 1)
                sp.dma_start(out_v[:, t, :], xs[:, t, :]).then_inc(out_done, 16)
            sp.wait_ge(out_done, 16 * NB)

        @block.gpsimd
        def _(pool):
            def split(dst_hi, dst_lo, src, hi_sem, hi_count, lo_sem):
                nc.gpsimd.tensor_copy(dst_hi, src).then_inc(hi_sem, 1)
                pool.wait_ge(hi_sem, hi_count)
                nc.gpsimd.tensor_tensor(dst_lo, src, f(dst_hi), ALU.subtract).then_inc(lo_sem, 1)

            nc.gpsimd.memset(mhalf[:, :, :], -0.5).then_inc(mhalf_set, 1)
            nc.gpsimd.memset(one[:, :], 1.0).then_inc(mhalf_set, 1)
            pool.wait_ge(in_kv, 32)
            nc.gpsimd.tensor_copy(wkv[:, :], rawkv).then_inc(wkv_hi, 1)
            pool.wait_ge(c_hi, 1)
            nc.gpsimd.tensor_tensor(cT[:, 1, :], rawc, f(cT[:, 0, :]), ALU.subtract).then_inc(c_split, 1)
            pool.wait_ge(eps1, 1)
            pool.wait_ge(mhalf_set, 2)
            nc.gpsimd.tensor_tensor(rstd[:, :, :], mv[:, :, 1:2], mhalf[:, :, :], ALU.pow).then_inc(rstd1, 1)
            pool.wait_ge(in_q, 16)
            split(wq[:, 0], wq[:, 1], rawq, wq_hi, 1, wq_split)
            nc.gpsimd.memset(f(kbd[:, 1, :, :, :]), 0.0).then_inc(kbd_zeroed, 1)
            nc.gpsimd.memset(vx[:, :, :, 3 * HD:VW], 1.0).then_inc(ones_set, 1)
            pool.wait_ge(in_o, 32)
            split(wo[:, 0], wo[:, 1], rawo, wo_hi, 1, wo_split)
            split(wr[:, 0], wr[:, 1], wrr[:, :, :], wr_hi, 1, wr_split)
            for pair in range(NB // 2):
                pool.wait_ge(job_lo, job("v", pair))
                r = vres[:, pair % 2, :].rearrange("p (g d) -> p g d", d=HD)
                v = vx[:, 2 * pair:2 * pair + 2, :, :].rearrange("p b h w -> p (b h) w")
                nc.gpsimd.tensor_copy(v[:, :, HD:2 * HD], r).then_inc(v2_done, 1)
                pool.wait_ge(v2_done, pair + 1)
                nc.gpsimd.tensor_tensor(v[:, :, 2 * HD:3 * HD], r, v[:, :, HD:2 * HD],
                                        ALU.subtract).then_inc(v3_done, 1)
            def split_piece(e, n, slot, count):
                part = slice(PIECE * n, PIECE * n + PIECE)
                src = stage[:, slot, part]
                hi = W[:, bass.ds(e, 1), 0, part].rearrange("p e w -> p (e w)")
                lo = W[:, bass.ds(e, 1), 1, part].rearrange("p e w -> p (e w)")
                nc.gpsimd.tensor_tensor(hi, src, one[:, :].to_broadcast([P, PIECE]), ALU.mult).then_inc(w_hi, 1)
                pool.wait_ge(w_hi, count)
                nc.gpsimd.tensor_tensor(lo, src, f(hi), ALU.subtract).then_inc(w_split, 1)

            def body(i, slots):
                for s in slots:
                    n = s - 2
                    half = n // PIECES
                    if 0 <= n < 2 * PIECES and (not isinstance(i, int) or 0 <= 2 * i - 1 + half < E):
                        e = 2 * i - 1 + half
                        if n == 0:
                            pool.wait_ge(in_w[0], 32 * i)
                            if not isinstance(i, int):
                                for u in range(2):
                                    pool.wait_ge(kq_loaded[u], PREFETCHES * (i + 1))
                        if n == PIECES:
                            pool.wait_ge(in_w[1], 32 * (i + 1))
                        split_piece(e, n % PIECES, half, PIECES * e + n % PIECES + 1)
                    if due(i, s, POW_LAG, GPB):
                        n = (s - POW_LAG) // GPB
                        u = n % 2
                        pool.wait_ge(eps2, 2 * i + n + 1)
                        nc.gpsimd.tensor_tensor(rstd2[:, u, :], mv2[:, u, 1:2], mhalf[:, 0, :],
                                                ALU.pow).then_inc(rstd2_done, 1)
            schedule(pool, body, NB // 2, TAIL)
            pool.wait_ge(idx_set, 2)
            for u in range(2):
                pool.wait_ge(xn_stored[u], 16 * NB // 2)

            def moe(i, slots):
                for s in slots:
                    if tile_due(i, s, 0):
                        if tile_past(i, s, 0, SLOTS):
                            pool.wait_ge(xgT_done, SLOTS * i + s - SLOTS)
                        nc.gpsimd.indirect_dma_start(xg[:, s, :], None, xnd,
                                                     bass.IndirectOffsetOnAxis(ap=idx[:, 0, SLOTS * i + s:SLOTS * i + s + 1], axis=0)
                                                     ).then_inc(xg_in[s], 16)
                    if tile_due(i, s, SEND_LAG):
                        n = (s - SEND_LAG) % SLOTS
                        pool.wait_ge(y_out, SLOTS * i + s - SEND_LAG)
                        j = SLOTS * i + s - SEND_LAG
                        nc.gpsimd.indirect_dma_start(yout, bass.IndirectOffsetOnAxis(ap=idx[:, 1, j:j + 1], axis=0),
                                                     ys[:, n, :], None).then_inc(y_sent[n], 16)
            for i in range(ROUNDS):
                moe(i, range(SLOTS))
            moe(ROUNDS, range(SEND_LAG))

        @block.scalar
        def _(act):
            act.wait_ge(in_c, 32)
            nc.scalar.copy(cT[:, 0, :], rawc).then_inc(c_hi, 1)
            for n, (kind, a, hf) in enumerate(JOBS):
                bank = ps[:, n % 8, :]
                act.wait_ge(job_done, n + 1)
                if kind == "k":
                    op = nc.scalar.copy(kT[:, a, bass.ts(hf, HALF)], bank)
                elif kind == "q":
                    op = nc.scalar.activation(qT[:, a, bass.ts(hf, HALF)], bank, ACT.Copy, scale=QSCALE)
                elif kind == "t":
                    op = nc.scalar.copy(xT[:, 0, :, bass.ts(a, 2 * P)], bank.rearrange("p (c t) -> p c t", c=KC))
                else:
                    v = vx[:, 2 * a:2 * a + 2, :, :].rearrange("p b h w -> p (b h) w")
                    op = nc.scalar.copy(v[:, :, 0:HD], bank.rearrange("p (g d) -> p g d", d=HD))
                op.then_inc(job_hi, 1)
            act.wait_ge(in_g, 32)
            nc.scalar.activation(tg[:, :], gate[:, :], ACT.Tanh).then_inc(tg_set, 1)

            def body(i, slots):
                for s in slots:
                    if due(i, s, EVICT_LAG):
                        n = s - EVICT_LAG
                        act.wait_ge(turned, SLOTS * i + n + 1)
                        if not isinstance(i, int) or SLOTS * i + n >= 2:
                            act.wait_ge(pv_done, SLOTS * i + n - 1)
                        nc.scalar.activation(pth[:, n % 2, :], ps[:, 2 + n % 2, :], ACT.Copy,
                                             scale=PSCALE).then_inc(pth_done, 1)
                    if due(i, s, 0):
                        act.wait_ge(negm_done, SLOTS * i + s + 1)
                        if not isinstance(i, int) or i > 0 or s >= 2:
                            act.wait_ge(turned, SLOTS * i + s - 1)
                        else:
                            act.wait_ge(v3_done, NB // 2)
                        for j in range(GH):
                            op = nc.scalar.activation(prob[:, s % 2, j * P:(j + 1) * P],
                                                      ps[:, s % 2, j * P:(j + 1) * P], ACT.Exp,
                                                      bias=negm[:, s % 2, j:j + 1])
                        op.then_inc(exp_done, 1)
                    if due(i, s, ATT_LO_LAG, GPB):
                        n = (s - ATT_LO_LAG) // GPB
                        act.wait_ge(attT_done, 2 * i + n + 1)
                        if not isinstance(i, int) or 2 * i + n >= 1:
                            act.wait_ge(oproj_done, 2 * i + n)
                        nc.scalar.copy(rT[:, 0, 0], ps[:, 6, 0:KC * P].rearrange("p (c t) -> p c t", c=KC)
                                       ).then_inc(attT_hi, 1)
                    if due(i, s, X2T_OUT_LAG, GPB):
                        n = (s - X2T_OUT_LAG) // GPB
                        act.wait_ge(x2T_done, 2 * i + n + 1)
                        nc.scalar.copy(xT[:, 0, :, bass.ts(2 * i + n, P)],
                                       ps[:, 6, 0:KC * P].rearrange("p (c t) -> p c t", c=KC)).then_inc(x2T_hi, 1)
                        act.dma_start(xnd[bass.ds((2 * i + n) * P, P), :], nrm[:, n % 2, :]
                                      ).then_inc(xn_stored[n % 2], 16)
            schedule(act, body, NB // 2, TAIL)

            for hf in range(2):
                act.wait_ge(rt_done, hf + 1)
                nc.scalar.copy(lgT[:, bass.ts(hf, HALF)], ps[0:E, hf, :]).then_inc(rt_out, 1)
            act.wait_ge(rt_exp_in, 1)
            nc.scalar.activation(pr[:, :, :], lg[:, :, :], ACT.Exp).then_inc(rt_exp, 1)
            nc.scalar.activation(junk[:, 0:1], gate[:, 0:1], ACT.Silu)

            def moe(i, slots):
                for s in slots:
                    if tile_due(i, s, X_LAG):
                        act.wait_ge(xgT_done, SLOTS * i + s)
                        if tile_past(i, s, X_LAG, 2):
                            act.wait_ge(gu_done, SLOTS * i + s - 2)
                        nc.scalar.copy(xT[:, 0, :, bass.ts(s % 2, P)], ps[:, s % 2, 0:D].rearrange("p (c t) -> p c t", c=KC)
                                       ).then_inc(xgT_hi, 1)
                    if tile_due(i, s, GU_LAG):
                        n = (s - GU_LAG) % 2
                        act.wait_ge(gu_done, SLOTS * i + s - GU_LAG)
                        if tile_past(i, s, GU_LAG, 2):
                            act.wait_ge(h_done, SLOTS * i + s - GU_LAG - 2)
                        nc.scalar.activation(sg[:, n, 0:D], ps[:, 2 + n, 0:D], ACT.Silu).then_inc(silu_done, 1)
                    if tile_due(i, s, H_LAG):
                        n = (s - H_LAG) % 2
                        act.wait_ge(hT_done, SLOTS * i + s - H_LAG)
                        if tile_past(i, s, H_LAG, 2):
                            act.wait_ge(y_done, SLOTS * i + s - H_LAG - 2)
                        nc.scalar.copy(rT[:, n, 0], ps[:, 4 + n, 0:D].rearrange("p (c t) -> p c t", c=KC)
                                       ).then_inc(hT_hi, 1)
                    if tile_due(i, s, Y_LAG):
                        n = (s - Y_LAG) % SLOTS
                        act.wait_ge(y_done, SLOTS * i + s - Y_LAG)
                        if tile_past(i, s, Y_LAG, SLOTS):
                            before_ = (s - Y_LAG) // SLOTS
                            act.wait_ge(y_sent[n], 16 * (i + before_ if n > 0 else i + before_ - 1))
                        nc.scalar.copy(ys[:, n, :], ps[:, 6 + n % 2, 0:D]).then_inc(y_out, 1)
            schedule(act, moe, ROUNDS, Y_LAG)

        @block.vector
        def _(dve):
            nc.vector.memset(f(kbd[:, 0, :, :, :]), 0.0).then_inc(kbd_zeroed, 1)
            for b in range(NB):
                if b % (NB // 2) == 0:
                    dve.wait_ge(in_x[b // (NB // 2)], 16)
                nc.vector.bn_stats(stat[:, b, :], xs[:, b, :]).then_inc(stats1, 1)
            dve.wait_ge(wkv_hi, 1)
            nc.vector.tensor_tensor(wkv[L:P, :], rawkv[L:P, :], f(wkv[L:P, :]), ALU.subtract).then_inc(wkv_split, 1)
            for b in range(NB):
                dve.wait_ge(stats1, b + 1)
                nc.vector.bn_aggr(mv[:, b, :], stat[:, b, :]).then_inc(aggr1, 1)
            dve.wait_ge(aggr1, NB)
            nc.vector.tensor_scalar(mv[:, :, 1:2], mv[:, :, 1:2], EPS, None, ALU.add).then_inc(eps1, 1)

            def job_low(n):
                kind, a, hf = JOBS[n]
                bank = ps[:, n % 8, :]
                dve.wait_ge(job_hi, n + 1)
                if kind == "k":
                    half = bass.ts(hf, HALF)
                    op = nc.vector.tensor_tensor(kT[:, KC + a, half], bank, f(kT[:, a, half]), ALU.subtract)
                elif kind == "q":
                    half = bass.ts(hf, HALF)
                    op = nc.vector.scalar_tensor_tensor(qT[:, KC + a, half], bank, QSCALE, f(qT[:, a, half]),
                                                        ALU.mult, ALU.subtract)
                elif kind == "t":
                    op = nc.vector.tensor_tensor(xT[:, 1, :, bass.ts(a, 2 * P)], bank.rearrange("p (c t) -> p c t", c=KC),
                                                 f(xT[:, 0, :, bass.ts(a, 2 * P)]), ALU.subtract)
                else:
                    if a >= 2:
                        dve.wait_ge(v3_done, a - 1)
                    v = vx[:, 2 * a:2 * a + 2, :, :].rearrange("p b h w -> p (b h) w")
                    op = nc.vector.tensor_tensor(vres[:, a % 2, :].rearrange("p (g d) -> p g d", d=HD),
                                                 bank.rearrange("p (g d) -> p g d", d=HD), v[:, :, 0:HD], ALU.subtract)
                op.then_inc(job_lo, 1)

            for n in range(KC):
                job_low(n)
            dve.wait_ge(rstd1, 1)
            for n in range(KC, len(JOBS)):
                kind, pair, _ = JOBS[n]
                if kind == "t" and pair % 2 == 0:
                    for b in range(2 * pair, 2 * pair + 4):
                        if b >= 4:
                            dve.wait_ge(job_done, job("t", b // 2 - 2))
                        nc.vector.tensor_scalar(nrm[:, b % 4, :], xs[:, b, :], mv[:, b, 0:1], rstd[:, b, :],
                                                ALU.subtract, ALU.mult).then_inc(norm1, 1)
                job_low(n)

            def body(i, slots):
                for s in slots:
                    if due(i, s, 0):
                        dve.wait_ge(scores_done, SLOTS * i + s + 1)
                        if not isinstance(i, int) or i > 0 or s >= 2:
                            dve.wait_ge(exp_done, SLOTS * i + s - 1)
                        nc.vector.tensor_reduce(negm[:, s % 2, :], ps[:, s % 2, :].rearrange("p (h k) -> p h k", h=GH),
                                                AX_X, ALU.max, negate=True).then_inc(negm_done, 1)
                    if due(i, s, EVICT_LAG):
                        n = s - EVICT_LAG
                        dve.wait_ge(pth_done, SLOTS * i + n + 1)
                        if not isinstance(i, int) or SLOTS * i + n >= 2:
                            dve.wait_ge(pv_done, SLOTS * i + n - 1)
                        nc.vector.scalar_tensor_tensor(ptl[:, n % 2, :], ps[:, 2 + n % 2, :], PSCALE,
                                                       pth[:, n % 2, :], ALU.mult, ALU.subtract).then_inc(ptl_done, 1)
                    for part, lag in ((0, HALF0_LAG), (1, HALF1_LAG)):
                        if due(i, s, lag, GPB):
                            n = (s - lag) // GPB
                            half = 2 * (2 * i + n) + part
                            bank = ps[:, 4 + part, :].rearrange("p (h w) -> p h w", w=64)
                            o = slice(P * part, P * part + P)
                            dve.wait_ge(pv_done, GPB * (2 * i + n) + 2 * part + 2)
                            nc.vector.tensor_reduce(attr[:, o].rearrange("p (h d) -> p h d", d=HD),
                                                    bank[:, :, 0:3 * HD].rearrange("p h (c d) -> p h d c", c=3),
                                                    AX_X, ALU.add).then_inc(sums_done, 1)
                            nc.vector.reciprocal(rinv[:, :].unsqueeze(2),
                                                 bank[:, :, 3 * HD:3 * HD + 1]).then_inc(sums_done, 1)
                            dve.wait_ge(sums_done, 2 * half + 2)
                            if not isinstance(i, int) or 2 * i + n >= 1:
                                dve.wait_ge(attT_done, 2 * i + n)
                            nc.vector.tensor_tensor(att[:, o].rearrange("p (h d) -> p h d", d=HD),
                                                    attr[:, o].rearrange("p (h d) -> p h d", d=HD),
                                                    rinv[:, :].unsqueeze(2).to_broadcast([P, HPC, HD]),
                                                    ALU.mult).then_inc(att_done, 1)
                    if due(i, s, NORM2_LAG, GPB):
                        n = (s - NORM2_LAG) // GPB
                        b, u = 2 * i + n, n % 2
                        dve.wait_ge(rstd2_done, b + 1)
                        if not isinstance(i, int) or b >= 2:
                            dve.wait_ge(x2T_done, b)
                            dve.wait_ge(xn_stored[u], 16 * (i + n // 2))
                        nc.vector.tensor_scalar(nrm[:, u, :], nrm[:, 2 + u, :], rstd2[:, u, :], None,
                                                ALU.mult).then_inc(norm2, 1)
                    if due(i, s, ATT_LO_LAG, GPB):
                        n = (s - ATT_LO_LAG) // GPB
                        dve.wait_ge(attT_hi, 2 * i + n + 1)
                        if not isinstance(i, int) or 2 * i + n >= 1:
                            dve.wait_ge(oproj_done, 2 * i + n)
                        nc.vector.tensor_tensor(rT[:, 0, 1], ps[:, 6, 0:KC * P].rearrange("p (c t) -> p c t", c=KC),
                                                f(rT[:, 0, 0]), ALU.subtract).then_inc(attT_lo, 1)
                    if due(i, s, X1_LAG, GPB):
                        n = (s - X1_LAG) // GPB
                        b, u = 2 * i + n, n % 2
                        xb = xs[:, bass.ds(b, 1), :].rearrange("p b d -> p (b d)")
                        dve.wait_ge(oproj_done, b + 1)
                        if isinstance(i, int) and 2 * i + n == 0:
                            dve.wait_ge(tg_set, 1)
                        nc.vector.scalar_tensor_tensor(xb, ps[:, 7, 0:D], tg[:, 0:1], xb, ALU.mult, ALU.add,
                                                       accum_out=mv2[:, u, 0:1]).then_inc(x1_done, 1)
                        dve.wait_ge(x1_done, b + 1)
                        nc.vector.tensor_scalar(mv2[:, u, 0:1], mv2[:, u, 0:1], 1.0 / D, None,
                                                ALU.mult).then_inc(mean2, 1)
                        dve.wait_ge(mean2, b + 1)
                        nc.vector.tensor_scalar(nrm[:, 2 + u, :], xb, mv2[:, u, 0:1], None,
                                                ALU.subtract).then_inc(centred2, 1)
                        dve.wait_ge(centred2, b + 1)
                        nc.vector.tensor_tensor_reduce(junk[:, :], nrm[:, 2 + u, :], nrm[:, 2 + u, :], 1.0, 0.0,
                                                       ALU.mult, ALU.add, mv2[:, u, 1:2]).then_inc(squares2, 1)
                        dve.wait_ge(squares2, b + 1)
                        nc.vector.tensor_scalar(mv2[:, u, 1:2], mv2[:, u, 1:2], 1.0 / D, EPS,
                                                ALU.mult, ALU.add).then_inc(eps2, 1)
                    if due(i, s, X2T_OUT_LAG, GPB):
                        n = (s - X2T_OUT_LAG) // GPB
                        b = 2 * i + n
                        dve.wait_ge(x2T_hi, b + 1)
                        nc.vector.tensor_tensor(xT[:, 1, :, bass.ts(b, P)],
                                                ps[:, 6, 0:KC * P].rearrange("p (c t) -> p c t", c=KC),
                                                f(xT[:, 0, :, bass.ts(b, P)]), ALU.subtract).then_inc(x2T_lo, 1)
            schedule(dve, body, NB // 2, TAIL)

            steps = [0]

            def step(ins):
                steps[0] += 1
                ins.then_inc(rt_step, 1)
                dve.wait_ge(rt_step, steps[0])

            def over_e(ap):
                return ap.unsqueeze(2).to_broadcast([P, NB, E])

            dve.wait_ge(rt_T, 1)
            step(nc.vector.tensor_copy(lg[:, :, :], ps[:, 2, 0:NB * E].rearrange("p (t e) -> p t e", e=E)))
            step(nc.vector.tensor_reduce(lmax[:, :], lg[:, :, :], AX_X, ALU.max))
            nc.vector.tensor_tensor(lg[:, :, :], lg[:, :, :], over_e(lmax[:, :]), ALU.subtract).then_inc(rt_exp_in, 1)
            dve.wait_ge(rt_exp, 1)
            step(nc.vector.tensor_reduce(psum_r[:, :], pr[:, :, :], AX_X, ALU.add))
            step(nc.vector.reciprocal(psum_r[:, :], psum_r[:, :]))
            step(nc.vector.tensor_tensor(pr[:, :, :], pr[:, :, :], over_e(psum_r[:, :]), ALU.mult))
            pj = pr[:, :, :].unsqueeze(2).to_broadcast([P, NB, E, E])
            pi = pr[:, :, :].unsqueeze(3).to_broadcast([P, NB, E, E])
            step(nc.vector.tensor_tensor(cmpa, pj, pi, ALU.is_gt))
            step(nc.vector.tensor_tensor(cmpb, pj, pi, ALU.is_equal))
            tri_v = tri.unsqueeze(1).to_broadcast([P, NB, E, E])
            step(nc.vector.tensor_tensor(cmpb, cmpb, tri_v, ALU.mult))
            step(nc.vector.tensor_tensor(cmpa, cmpa, cmpb, ALU.add))
            step(nc.vector.tensor_reduce(rank[:, :, :], cmpa, AX_X, ALU.add))
            nc.vector.tensor_scalar(chosen[:, :, :], rank[:, :, :], float(TOPK), None, ALU.is_lt).then_inc(chosen_set, 1)
            for k in range(TOPK):
                step(nc.vector.tensor_scalar(choice[:, k], rank[:, :, :], float(k), None, ALU.is_equal))
            def over_k(ap):
                return ap.unsqueeze(1).to_broadcast([P, TOPK, NB, E])
            dve.wait_ge(counted, 1)
            step(nc.vector.tensor_tensor(picked, choice, over_k(ps[:, 3, 0:NB * E].rearrange("p (t e) -> p t e", e=E)),
                                         ALU.mult))
            step(nc.vector.tensor_reduce(rank_k.rearrange("p (k t) -> p k t", k=TOPK), picked, AX_X, ALU.add))
            step(nc.vector.tensor_scalar(over, rank_k, -(P - 1) / 2, 1.0 / P, ALU.add, ALU.mult))
            step(nc.vector.tensor_scalar(over, over, ROUND, None, ALU.add))
            step(nc.vector.tensor_scalar(nfull, over, -ROUND, None, ALU.add))
            step(nc.vector.scalar_tensor_tensor(place, nfull, -float(P), rank_k, ALU.mult, ALU.add))
            nc.vector.tensor_tensor(at_place, place.unsqueeze(2).to_broadcast([P, TOPK * NB, P]),
                                    col_no.unsqueeze(1).to_broadcast([P, TOPK * NB, P]), ALU.is_equal
                                    ).then_inc(sorted_in, 1)
            count = ps[:, 3, NB * E:NB * E + E].unsqueeze(2).to_broadcast([P, E, NB])
            step(nc.vector.tensor_tensor(full, count, fulls, ALU.is_gt))
            step(nc.vector.tensor_reduce(ntiles, full, AX_X, ALU.add))
            step(nc.vector.tensor_tensor(cum, ntiles.unsqueeze(1).to_broadcast([P, E, E]), upto, ALU.mult))
            step(nc.vector.tensor_reduce(cum_end, cum, AX_X, ALU.add))
            step(nc.vector.tensor_tensor(cum_start, cum_end, ntiles, ALU.subtract))
            step(nc.vector.tensor_tensor(picked.rearrange("p k t e -> p (k t) e"), choice.rearrange("p k t e -> p (k t) e"),
                                         cum_start.unsqueeze(1).to_broadcast([P, TOPK * NB, E]), ALU.mult))
            step(nc.vector.tensor_reduce(tile_k.rearrange("p (k t) -> p k t", k=TOPK), picked, AX_X, ALU.add))
            step(nc.vector.tensor_tensor(tile_k, tile_k, nfull, ALU.add))
            step(nc.vector.tensor_tensor(in_tile, tile_k.unsqueeze(2).to_broadcast([P, TOPK * NB, J]),
                                         tile_no.unsqueeze(1).to_broadcast([P, TOPK * NB, J]), ALU.is_equal))
            nc.vector.tensor_scalar(at_tile[:, :, 0, :], in_tile, part_no, None, ALU.mult).then_inc(sorted_in, 1)
            nc.vector.tensor_tensor(at_tile[:, :, 1, :], in_tile, block_no.unsqueeze(2).to_broadcast([P, TOPK * NB, J]),
                                    ALU.mult).then_inc(sorted_in, 1)
            step(nc.vector.tensor_tensor(past, cum_end.unsqueeze(1).to_broadcast([P, J, E]),
                                         tile_no.unsqueeze(2).to_broadcast([P, J, E]), ALU.is_le))
            step(nc.vector.tensor_reduce(tile_e, past, AX_X, ALU.add))
            nc.vector.tensor_scalar(tile_expert[:, :], tile_e, float(E - 1), None, ALU.min).then_inc(experts_set, 1)
            dve.wait_ge(sorted_out, 1)
            part, blk = ps[:, 2, 0:J], ps[:, 2, J:2 * J]
            step(nc.vector.tensor_copy(v1, part))
            step(nc.vector.scalar_tensor_tensor(v1, blk, float(P), v1, ALU.mult, ALU.add))
            step(nc.vector.tensor_scalar(c0, v1, float(P + NTOK), -float(NTOK), ALU.is_ge, ALU.mult))
            step(nc.vector.scalar_tensor_tensor(c0, v1, -float(P), c0, ALU.add, ALU.add))
            nc.vector.tensor_scalar(idx[:, 0, :], c0, 0.0, None, ALU.max).then_inc(idx_set, 1)
            step(nc.vector.scalar_tensor_tensor(e0, v1, 0.0, empty_row, ALU.is_equal, ALU.mult))
            nc.vector.scalar_tensor_tensor(idx[:, 1, :], v1, -float(P), e0, ALU.add, ALU.add).then_inc(idx_set, 1)

            step(nc.vector.tensor_tensor(picked, choice, over_k(pr[:, :, :]), ALU.mult))
            step(nc.vector.tensor_reduce(wk, picked, AX_X, ALU.add))
            step(nc.vector.tensor_tensor(psum_r[:, :], wk[:, 0], wk[:, 1], ALU.add))
            step(nc.vector.reciprocal(psum_r[:, :], psum_r[:, :]))
            step(nc.vector.tensor_scalar(psum_r[:, :], psum_r[:, :], tg[:, 1:2], None, ALU.mult))
            step(nc.vector.tensor_tensor(wk, wk, psum_r[:, :].unsqueeze(1).to_broadcast([P, TOPK, NB]), ALU.mult))

            def moe(i, slots):
                for s in slots:
                    if tile_due(i, s, X_LAG):
                        dve.wait_ge(xgT_hi, SLOTS * i + s)
                        if tile_past(i, s, X_LAG, 2):
                            dve.wait_ge(gu_done, SLOTS * i + s - 2)
                        nc.vector.tensor_tensor(xT[:, 1, :, bass.ts(s % 2, P)],
                                                ps[:, s % 2, 0:D].rearrange("p (c t) -> p c t", c=KC),
                                                f(xT[:, 0, :, bass.ts(s % 2, P)]), ALU.subtract).then_inc(xgT_lo, 1)
                    if tile_due(i, s, GU_LAG):
                        n = (s - GU_LAG) % 2
                        dve.wait_ge(silu_done, SLOTS * i + s - GU_LAG)
                        if tile_past(i, s, GU_LAG, 2):
                            dve.wait_ge(hT_done, SLOTS * i + s - GU_LAG - 2)
                        nc.vector.tensor_tensor(h[:, n, :], ps[:, 2 + n, D:2 * D], sg[:, n, 0:D],
                                                ALU.mult).then_inc(h_done, 1)
                    if tile_due(i, s, H_LAG):
                        n = (s - H_LAG) % 2
                        dve.wait_ge(hT_hi, SLOTS * i + s - H_LAG)
                        if tile_past(i, s, H_LAG, 2):
                            dve.wait_ge(y_done, SLOTS * i + s - H_LAG - 2)
                        nc.vector.tensor_tensor(rT[:, n, 1], ps[:, 4 + n, 0:D].rearrange("p (c t) -> p c t", c=KC),
                                                f(rT[:, n, 0]), ALU.subtract).then_inc(hT_lo, 1)
            for u in range(2):
                dve.wait_ge(xn_stored[u], 16 * NB // 2)
            schedule(dve, moe, ROUNDS, H_LAG)

            for t in range(NB):
                q = t // (NB // 2)
                for k, done in enumerate((add0_done, add1_done)):
                    if t % (NB // 2) == 0:
                        dve.wait_ge(yk_in[k][q], 16)
                    if k == 1:
                        dve.wait_ge(add0_done, t + 1)
                    nc.vector.scalar_tensor_tensor(xs[:, t, :], yk[:, k, t, :], wk[:, k, t:t + 1], xs[:, t, :],
                                                   ALU.mult, ALU.add).then_inc(done, 1)

        @block.tensor
        def _(pe):
            def mm3(out_, a_hi, a_lo, b_hi, b_lo, first, last):
                nc.tensor.matmul(out_, a_hi, b_hi, start=first, stop=False)
                nc.tensor.matmul(out_, a_hi, b_lo, start=False, stop=False)
                return nc.tensor.matmul(out_, a_lo, b_hi, start=False, stop=last)

            for n, (kind, a, hf) in enumerate(JOBS):
                bank = ps[:, n % 8, :]
                half = bass.ts(hf, HALF)
                if n == 0:
                    pe.wait_ge(wkv_split, 1)
                    pe.wait_ge(c_split, 1)
                if n >= 8:
                    pe.wait_ge(job_lo, n - 7)
                if kind == "k":
                    w = wkv[:, a * P:(a + 1) * P]
                    nc.tensor.matmul(bank, w, cT[:, 0, half], start=True, stop=False)
                    mm = nc.tensor.matmul(bank, w, cT[:, 1, half], start=False, stop=True)
                elif kind == "v":
                    for u in range(2):
                        o = bank[:, D * u:D * u + D]
                        tok = bass.ts(2 * a + u, P)
                        nc.tensor.matmul(o, cT[:, 0, tok], wkv[:, D:2 * D], start=True, stop=False)
                        mm = nc.tensor.matmul(o, cT[:, 1, tok], wkv[:, D:2 * D], start=False, stop=True)
                elif kind == "t":
                    pe.wait_ge(in_const, 32)
                    pe.wait_ge(norm1, 2 * a + 2)
                    for u in range(2):
                        for c in range(KC):
                            mm = nc.tensor.transpose(bank[:, 2 * P * c + P * u:2 * P * c + P * u + P],
                                                     nrm[:, (2 * a + u) % 4, c * P:(c + 1) * P], identf)
                else:
                    pe.wait_ge(wq_split, 1)
                    pe.wait_ge(job_lo, job("t", 2 * hf + 1))
                    for c in range(KC):
                        m = slice(a * P, (a + 1) * P)
                        mm = mm3(bank, wq[:, 0, c, m], wq[:, 1, c, m], xT[:, 0, c, half], xT[:, 1, c, half],
                                 c == 0, c == KC - 1)
                mm.then_inc(job_done, 1)

            pe.wait_ge(job_lo, len(JOBS))
            pe.wait_ge(ones_set, 1)
            pe.wait_ge(v3_done, NB // 2)
            pe.wait_ge(wo_split, 1)

            def body(i, slots):
                for s in slots:
                    if due(i, s, 0):
                        u, g = s // GPB, s % GPB
                        c, j0 = g // 2, GH * (g % 2)
                        if g == 0:
                            pe.wait_ge(kq_loaded[u], PREFETCHES * (i + 1))
                        if not isinstance(i, int) or i > 0 or s >= 2:
                            pe.wait_ge(exp_done, SLOTS * i + s - 1)
                        bank = ps[:, s % 2, :]

                        def keys(part):
                            return kbd[:, u, KC * part + c, j0:j0 + GH, :].rearrange("p h k -> p (h k)")
                        nc.tensor.matmul(bank.rearrange("p (h k) -> p h k", h=GH), identb,
                                         mask.unsqueeze(1).to_broadcast([P, GH, P]),
                                         start=True, stop=False)
                        mm3(bank, qb[:, u, c, :], qb[:, u, KC + c, :], keys(0), keys(1), False, True
                            ).then_inc(scores_done, 1)
                    if due(i, s, TURN_LAG):
                        n = s - TURN_LAG
                        pe.wait_ge(exp_done, SLOTS * i + n + 1)
                        if not isinstance(i, int) or SLOTS * i + n >= 2:
                            pe.wait_ge(ptl_done, SLOTS * i + n - 1)
                        for j in range(GH):
                            mm = nc.tensor.transpose(ps[:, 2 + n % 2, j * P:(j + 1) * P],
                                                     prob[:, n % 2, j * P:(j + 1) * P], identf)
                        mm.then_inc(turned, 1)
                    if due(i, s, PV_LAG):
                        n = s - PV_LAG
                        g = n % GPB
                        b = 2 * i + n // GPB
                        pe.wait_ge(ptl_done, SLOTS * i + n + 1)
                        if g % 2 == 0 and (not isinstance(i, int) or 2 * i + n // GPB >= 1):
                            pe.wait_ge(sums_done, 4 * (b - 1) + g + 2)
                        for j in range(GH):
                            hh = GH * (g % 2) + j
                            o = ps[:, 4 + g // 2, 64 * hh:64 * hh + 3 * HD + 1]
                            v = vx[:, bass.ds(b, 1), GH * g + j, 0:3 * HD + 1].rearrange("p b w -> p (b w)")
                            nc.tensor.matmul(o, pth[:, n % 2, j * P:(j + 1) * P], v, start=True, stop=False)
                            mm = nc.tensor.matmul(o, ptl[:, n % 2, j * P:(j + 1) * P], v, start=False, stop=True)
                        mm.then_inc(pv_done, 1)
                    if due(i, s, ATT_T_LAG, GPB):
                        n = (s - ATT_T_LAG) // GPB
                        b = 2 * i + n
                        pe.wait_ge(att_done, 2 * b + 2)
                        if not isinstance(i, int) or b >= 1:
                            pe.wait_ge(x2T_lo, b)
                        for c in range(KC):
                            mm = nc.tensor.transpose(ps[:, 6, c * P:(c + 1) * P], att[:, c * P:(c + 1) * P], identf)
                        mm.then_inc(attT_done, 1)
                    if due(i, s, OPROJ_LAG, GPB):
                        n = (s - OPROJ_LAG) // GPB
                        b = 2 * i + n
                        pe.wait_ge(attT_lo, b + 1)
                        if not isinstance(i, int) or b >= 1:
                            pe.wait_ge(x1_done, b)
                        for c in range(KC):
                            mm = mm3(ps[:, 7, 0:D], rT[:, 0, 0, c, :], rT[:, 0, 1, c, :], wo[:, 0, c, :], wo[:, 1, c, :],
                                     c == 0, c == KC - 1)
                        mm.then_inc(oproj_done, 1)
                    if due(i, s, X2T_LAG, GPB):
                        n = (s - X2T_LAG) // GPB
                        b, u = 2 * i + n, n % 2
                        pe.wait_ge(norm2, b + 1)
                        pe.wait_ge(attT_lo, b + 1)
                        for c in range(KC):
                            mm = nc.tensor.transpose(ps[:, 6, c * P:(c + 1) * P], nrm[:, u, c * P:(c + 1) * P],
                                                     identf)
                        mm.then_inc(x2T_done, 1)
            schedule(pe, body, NB // 2, TAIL)

            pe.wait_ge(x2T_lo, NB)
            pe.wait_ge(wr_split, 1)
            for hf in range(2):
                half = bass.ts(hf, HALF)
                for c in range(KC):
                    mm = mm3(ps[0:E, hf, :], wr[:, 0, c, :], wr[:, 1, c, :], xT[:, 0, c, half], xT[:, 1, c, half],
                             c == 0, c == KC - 1)
                mm.then_inc(rt_done, 1)
            pe.wait_ge(rt_out, 2)
            for t in range(NB):
                mm = nc.tensor.transpose(ps[:, 2, E * t:E * t + E], lgT[:, t * P:(t + 1) * P], identf[0:E, 0:E])
            mm.then_inc(rt_T, 1)

            pe.wait_ge(chosen_set, 1)
            pe.wait_ge(rt_step, 1)
            nc.tensor.matmul(ps[:, 3, 0:NB * E], before, chosen[:, :, :].rearrange("p t e -> p (t e)"),
                             start=True, stop=False)
            for t in range(NB - 1):
                nc.tensor.matmul(ps[:, 3, (t + 1) * E:NB * E].rearrange("p (t e) -> p t e", e=E), ones,
                                 chosen[:, t:t + 1, :].to_broadcast([P, NB - 1 - t, E]),
                                 start=False, stop=t == NB - 2)
            for t in range(NB):
                mm = nc.tensor.matmul(ps[:, 3, NB * E:NB * E + E], ones, chosen[:, t, :], start=t == 0, stop=t == NB - 1)
            mm.then_inc(counted, 1)

            pe.wait_ge(sorted_in, 3)
            M = TOPK * NB
            for m in range(M):
                mm = nc.tensor.matmul(ps[:, 2, 0:2 * J], at_place[:, m, :], at_tile[:, m, :, :].rearrange("p v j -> p (v j)"),
                                      start=m == 0, stop=m == M - 1)
            mm.then_inc(sorted_out, 1)

            pe.wait_ge(w_split, PIECES * E)
            pe.wait_ge(experts_set, 1)
            pe.wait_ge(idx_set, 2)

            def expert(i, s):
                at = tile_expert[0:1, SLOTS * i + s:SLOTS * i + s + 1] if isinstance(i, int) else \
                    tile_expert[0:1, bass.ds(SLOTS * i + s, 1)]
                return pe.value_load(at, min_val=0, max_val=E - 1)

            def moe(i, slots):
                for s in slots:
                    if tile_due(i, s, X_LAG):
                        pe.wait_ge(xg_in[s], 16 * (i + 1 if s > 0 else i))
                        if tile_past(i, s, X_LAG, 2):
                            pe.wait_ge(xgT_lo, SLOTS * i + s - 2)
                        for c in range(KC):
                            mm = nc.tensor.transpose(ps[:, s % 2, c * P:(c + 1) * P], xg[:, s, c * P:(c + 1) * P], identf)
                        mm.then_inc(xgT_done, 1)
                    if tile_due(i, s, GU_LAG):
                        n = (s - GU_LAG) % 2
                        e = expert(i, s - GU_LAG)
                        pe.wait_ge(xgT_lo, SLOTS * i + s - GU_LAG)
                        if tile_past(i, s, GU_LAG, 2):
                            pe.wait_ge(h_done, SLOTS * i + s - GU_LAG - 2)
                        for c in range(KC):
                            def w(part):
                                return W[:, bass.ds(e, 1), part, c * F2:(c + 1) * F2].rearrange("p e w -> p (e w)")
                            tok = slice(n * P, n * P + P)
                            mm = mm3(ps[:, 2 + n, :], xT[:, 0, c, tok], xT[:, 1, c, tok], w(0), w(1), c == 0, c == KC - 1)
                        mm.then_inc(gu_done, 1)
                    if tile_due(i, s, H_LAG):
                        n = (s - H_LAG) % 2
                        pe.wait_ge(h_done, SLOTS * i + s - H_LAG)
                        if tile_past(i, s, H_LAG, 2):
                            pe.wait_ge(hT_lo, SLOTS * i + s - H_LAG - 2)
                        for c in range(KC):
                            mm = nc.tensor.transpose(ps[:, 4 + n, c * P:(c + 1) * P], h[:, n, c * P:(c + 1) * P], identf)
                        mm.then_inc(hT_done, 1)
                    if tile_due(i, s, Y_LAG):
                        n = (s - Y_LAG) % 2
                        e = expert(i, s - Y_LAG)
                        pe.wait_ge(hT_lo, SLOTS * i + s - Y_LAG)
                        if tile_past(i, s, Y_LAG, 2):
                            pe.wait_ge(y_out, SLOTS * i + s - Y_LAG - 2)
                        for c in range(KC):
                            def w(part):
                                at = KC * F2 + c * D
                                return W[:, bass.ds(e, 1), part, at:at + D].rearrange("p e w -> p (e w)")
                            mm = mm3(ps[:, 6 + n, 0:D], rT[:, n, 0, c, :], rT[:, n, 1, c, :], w(0), w(1),
                                     c == 0, c == KC - 1)
                        mm.then_inc(y_done, 1)
            schedule(pe, moe, ROUNDS, Y_LAG)


def kernel(x, ctx_512, g_xattn, g_ffn, L0_xattn_Wq, L0_xattn_Wkv_expand, L0_xattn_Wout, L0_ffn_Wr, L0_ffn_Wg,
           L0_ffn_Wu, L0_ffn_Wd):
    import numpy as np
    import ml_dtypes
    import concourse.bacc as bacc
    from concourse import mybir
    from concourse.bass_utils import run_bass_kernel_spmd

    B, S, D = x.shape
    arrays = {
        "x": np.asarray(x).reshape(B * S, D),
        "ctxT": np.asarray(ctx_512).reshape(B * S, -1).T,
        "g_attn": np.asarray(g_xattn),
        "g_ffn": np.asarray(g_ffn),
        "WqT": np.asarray(L0_xattn_Wq).T,
        "WkvT": np.asarray(L0_xattn_Wkv_expand).T,
        "WoT": np.asarray(L0_xattn_Wout).T,
        "Wr": np.asarray(L0_ffn_Wr),
        "Wgu": np.concatenate([np.asarray(L0_ffn_Wg), np.asarray(L0_ffn_Wu)], axis=2),
        "Wd": np.asarray(L0_ffn_Wd),
    }
    T, E = B * S, L0_ffn_Wr.shape[1]
    NB, K = T // P, 2
    J = K * NB + E
    e, p, tile = np.arange(E), np.arange(P), np.arange(J) - 1

    def rows(a):
        return np.broadcast_to(a.reshape(1, -1), (P, a.size))
    arrays["consts"] = np.concatenate([
        np.eye(P),
        rows(P * np.arange(NB)),
        rows(e[None, :] <= e[:, None]), rows(e[None, :] < e[:, None]),
        rows(tile), p[:, None],
        rows(1 + np.arange(K * NB)),
        P + K * T + P * tile[None, :] + p[:, None],
    ], axis=1).astype(np.float32)
    arrays["consts16"] = np.concatenate(
        [np.where(p[None, :] <= p[:, None], 0.0, MASKED), np.eye(P), p[:, None] < p[None, :], np.ones((P, P)), rows(p)],
        axis=1).astype(ml_dtypes.bfloat16)
    arrays = {n: np.ascontiguousarray(a) for n, a in arrays.items()}
    nc = bacc.Bacc("TRN2", target_bir_lowering=False, num_devices=1)
    args = [nc.dram_tensor(n, a.shape, mybir.dt.from_np(a.dtype), kind="ExternalInput").ap() for n, a in arrays.items()]
    out = nc.dram_tensor("out", (B * S, D), mybir.dt.float32, kind="ExternalOutput").ap()
    build_gated_block(nc, *args, out)
    r = run_bass_kernel_spmd(nc, [arrays], core_ids=[0])
    return r.results[0]["out"].reshape(B, S, D)
```

```python
from contextlib import ExitStack

import concourse.bass as bass
from concourse import mybir

ALU = mybir.AluOpType
ACT = mybir.ActivationFunctionType
AX_X = mybir.AxisListType.X
F32 = mybir.dt.float32
F32R = mybir.dt.float32r
BF16 = mybir.dt.bfloat16
F16 = mybir.dt.float16
U32 = mybir.dt.uint32

P = 128
MASKED = -3.0e38
EPS = 1e-5


def build_gated_block(nc, x, ctxT, g_attn, g_ffn, WqT, WkvT, WoT, Wr, Wgu, Wd, consts, consts16, out):
    NTOK, D = x.shape
    L = ctxT.shape[0]
    NB = NTOK // P
    KC = D // P
    HD = 16
    NH = D // HD
    HPC = P // HD
    E, _, F2 = Wgu.shape
    GH = 4
    GPB = NH // GH
    NG = NB * GPB
    SLOTS = 2 * GPB
    VW = 3 * HD + 2
    BANK = 512
    WPE = KC * F2 + KC * D
    PIECE = 512
    PIECES = WPE // PIECE
    TOPK = 2
    NTILES = TOPK * NB + E - 1
    ROUNDS = (NTILES + 1) // SLOTS
    QSCALE = HD ** -0.5
    PSCALE = 4096.0
    ROUND = 1.5 * 2.0 ** 23
    assert L * 2 == P and D == KC * P and F2 == 2 * D and NB == 8 and E == 8 and (NTILES + 1) % SLOTS == 0

    with ExitStack() as ctx:
        def sb(name, shape, dt=F32):
            return ctx.enter_context(nc.sbuf_tensor(name, shape, dt))

        def sem(name):
            return ctx.enter_context(nc.semaphore(name))

        ps = ctx.enter_context(nc.psum_tensor("ps", [P, 8, BANK], F32))

        xs = sb("xs", [P, NB, D])
        nrm = sb("nrm", [P, 4, D])
        xT = sb("xT", [P, 2, KC, NTOK], F32R)
        kbd = sb("kbd", [P, 2, 4, HPC, P], F32R)
        qb = sb("qb", [P, 2, 4, P], F32R)
        vx = sb("vx", [P, NB, NH, VW], BF16)
        W = sb("W", [P, E, 2, WPE], F32R)
        stage = sb("stage", [P, 2, WPE])
        prob = sb("prob", [P, 2, BANK])
        pth = sb("pth", [P, 2, BANK], F16)
        ptl = sb("ptl", [P, 2, BANK], F16)
        attr = sb("attr", [P, D])
        att = sb("att", [P, D])
        rT = sb("rT", [P, 2, 2, KC, P], F32R)
        wo = sb("wo", [P, 2, KC, D], F32R)
        wrr = sb("wrr", [P, KC, E])
        wr = sb("wr", [P, 2, KC, E], F32R)
        cst = sb("cst", list(consts.shape))
        cst16 = sb("cst16", list(consts16.shape), BF16)
        nm2 = sb("nm2", [P, 2, 1])
        stat = sb("stat", [P, NB, 6])
        mv = sb("mv", [P, NB, 2])
        rstd = sb("rstd", [P, NB, 1])
        junk = sb("junk", [P, D], BF16)
        mv2 = sb("mv2", [P, 2, 2])
        rstd2 = sb("rstd2", [P, 2, 1])
        mhalf = sb("mhalf", [P, NB, 1])
        one = sb("one", [P, 1])
        unused = sb("unused", [P, 7 + 2 * SLOTS])
        negm = sb("negm", [P, 2, GH])
        rinv = sb("rinv", [P, HPC])
        gate = sb("gate", [P, 2])
        tg = sb("tg", [P, 2])
        lg = sb("lg", [P, NB, E])
        lmax = sb("lmax", [P, NB])
        pr = sb("pr", [P, NB, E])
        psum_r = sb("psum_r", [P, NB])
        order = sb("order", [P, NB, E])
        chosen = sb("chosen", [P, NB, E], BF16)
        J = NTILES + 1
        tile_expert = sb("tile_expert", [P, J], U32)
        idx = sb("idx", [P, 2, J], U32)
        xnd = nc.dram_tensor("xnd", (NTOK, D), F32, kind="Internal").ap()
        yout = nc.dram_tensor("yout", (TOPK * NTOK + NTILES * P, D), F32, kind="Internal").ap()

        cuts = [0]

        def const(n):
            cuts[0] += n
            return cst[:, cuts[0] - n:cuts[0]]
        identf = const(P)
        fulls = const(NB).unsqueeze(1).to_broadcast([P, E, NB])
        upto = const(E * E).rearrange("p (e j) -> p e j", e=E)
        falling = const(E)
        tile_no = const(J)
        d_eps, root_d = const(1), const(1)
        part_no = const(1)
        block_no = const(TOPK * NB)
        empty_row = const(J)
        mask, identb, before, ones, col_no = (cst16[:, P * k:P * k + P] for k in range(5))

        late = W[:, 5:E, :, :].rearrange("p e h w -> p (e h w)")
        NQ = 4 * NTOK
        qT = late[:, 0:NQ].rearrange("p (a t) -> p a t", a=4)
        kT = late[:, NQ:2 * NQ].rearrange("p (a t) -> p a t", a=4)
        at = 2 * NQ
        wq = late[:, at:at + 2 * KC * D].rearrange("p (a c n) -> p a c n", a=2, c=KC)
        late = W[:, 4, :, :].rearrange("p h w -> p (h w)")
        cT = late[:, 0:2 * NTOK].rearrange("p (a t) -> p a t", a=2)
        at = 2 * NTOK
        wkv = late[:, at:at + 2 * D]
        rawq = stage[:, 0, 0:512].rearrange("p (c n) -> p c n", c=KC)
        rawo = stage[:, 0, 512:1024].rearrange("p (c n) -> p c n", c=KC)
        rawkv = stage[:, 0, 1024:1536]
        rawc = stage[:, 1, 0:NTOK]
        vres = prob
        sg = prob
        h = nrm

        lgT = prob[0:E, :, :].rearrange("p a n -> p (a n)")
        scr = vx[:, NB // 2:NB, :, :].rearrange("p b h w -> p (b h w)").bitcast(F32)
        scr_cuts = [0]

        def scratch(n):
            scr_cuts[0] += n
            return scr[:, scr_cuts[0] - n:scr_cuts[0]]
        choice = scratch(TOPK * NB * E).rearrange("p (k t e) -> p k t e", k=TOPK, t=NB)
        picked = scratch(TOPK * NB * E).rearrange("p (k t e) -> p k t e", k=TOPK, t=NB)
        wk = scratch(TOPK * NB).rearrange("p (k t) -> p k t", k=TOPK)
        rank_k = scratch(TOPK * NB)
        over = scratch(TOPK * NB)
        nfull = scratch(TOPK * NB)
        place = scratch(TOPK * NB)
        tile_k = scratch(TOPK * NB)
        full = scratch(E * NB).rearrange("p (e k) -> p e k", e=E)
        ntiles = scratch(E)
        cum = scratch(E * E).rearrange("p (e j) -> p e j", e=E)
        cum_end, cum_start = scratch(E), scratch(E)
        past = scratch(J * E).rearrange("p (j e) -> p j e", e=E)
        tile_e, v1, e0, c0 = (scratch(J) for _ in range(4))
        in_tile = scratch(TOPK * NB * J).rearrange("p (m j) -> p m j", j=J)
        vflat = vx[:, 0:NB // 2, :, :].rearrange("p b h w -> p (b h w)")
        NA = TOPK * NB * P
        at_place = vflat[:, 0:NA].rearrange("p (m q) -> p m q", q=P)
        at_tile = vflat[:, NA:NA + TOPK * NB * 2 * J].rearrange("p (m v j) -> p m v j", v=2, j=J)
        kflat = kbd[:, :, :, :, :].rearrange("p u a h k -> p (u a h k)").bitcast(F32)
        xg = kflat[:, 0:SLOTS * D].rearrange("p (s d) -> p s d", d=D)
        yk = kflat[:, SLOTS * D:(SLOTS + TOPK * NB) * D].rearrange("p (k t d) -> p k t d", k=TOPK, d=D)
        ys = stage[:, :, :].rearrange("p s w -> p (s w)")[:, 0:SLOTS * D].rearrange("p (s d) -> p s d", d=D)

        def f(ap):
            return ap.bitcast(F32)

        in_x = [sem(f"in_x{i}") for i in range(2)]
        in_kv, in_c, in_q, in_o, in_g = (sem("in_" + n) for n in ("kv", "c", "q", "o", "g"))
        in_const = sem("in_const")
        ones_set, mhalf_set = sem("ones_set"), sem("mhalf_set")
        kbd_zeroed = [sem(f"kbd_zeroed{u}") for u in range(2)]
        wkv_hi, wkv_split, c_hi, c_split = (sem(n) for n in ("wkv_hi", "wkv_split", "c_hi", "c_split"))
        wq_hi, wq_split, wo_hi, wo_split, wr_hi, wr_split = (
            sem(n) for n in ("wq_hi", "wq_split", "wo_hi", "wo_split", "wr_hi", "wr_split"))
        stats1, aggr1, eps1, rstd1, norm1 = (sem(n) for n in ("stats1", "aggr1", "eps1", "rstd1", "norm1"))
        job_done, job_hi, job_lo, v2_done, v3_done = (
            sem(n) for n in ("job_done", "job_hi", "job_lo", "v2_done", "v3_done"))
        tg_set = sem("tg_set")
        kq_loaded = [sem(f"kq_loaded{u}") for u in range(2)]
        scores_done, negm_done, exp_done, turned, pth_done, ptl_done, pv_done = (
            sem(n) for n in ("scores_done", "negm_done", "exp_done", "turned", "pth_done", "ptl_done", "pv_done"))
        sums_done, att_done, attT_done, attT_hi, attT_lo, oproj_done, x1_done = (
            sem(n) for n in ("sums_done", "att_done", "attT_done", "attT_hi", "attT_lo", "oproj_done", "x1_done"))
        mean2, squares2, eps2, rsum2, rstd2_done, norm2, x2T_done, x2T_hi, x2T_lo = (
            sem(n) for n in ("mean2", "squares2", "eps2", "rsum2", "rstd2_done", "norm2", "x2T_done", "x2T_hi", "x2T_lo"))
        in_w, w_hi, w_split = [sem("in_w0"), sem("in_w1")], sem("w_hi"), sem("w_split")
        rt_done, rt_out, rt_T, rt_step, rt_exp_in, rt_exp = (
            sem(n) for n in ("rt_done", "rt_out", "rt_T", "rt_step", "rt_exp_in", "rt_exp"))
        xn_stored = [sem(f"xn_stored{u}") for u in range(2)]
        place_set, distance_set = sem("place_set"), sem("distance_set")
        chosen_set, counted, sorted_in, sorted_out, idx_set, experts_set = (
            sem(n) for n in ("chosen_set", "counted", "sorted_in", "sorted_out", "idx_set", "experts_set"))
        xg_in = [sem(f"xg_in{s}") for s in range(SLOTS)]
        y_sent = [sem(f"y_sent{s}") for s in range(SLOTS)]
        ys_free = sem("ys_free")
        xgT_done, xgT_hi, xgT_lo = sem("xgT_done"), sem("xgT_hi"), sem("xgT_lo")
        gu_done, silu_done, h_done, hT_done, hT_hi, hT_lo, y_done, y_out = (
            sem(n) for n in ("gu_done", "silu_done", "h_done", "hT_done", "hT_hi", "hT_lo", "y_done", "y_out"))
        yk_in = [[sem(f"yk_in{k}{q}") for q in range(3)] for k in range(TOPK)]
        add0_done, weighted = sem("add0_done"), sem("weighted")
        add1_done, last_done = sem("add1_done"), sem("last_done")
        out_done = sem("out_done")

        x_v = x.rearrange("(b p) d -> p b d", p=P)
        out_v = out.rearrange("(b p) d -> p b d", p=P)
        TURN_LAG, EVICT_LAG, PV_LAG, HALF0_LAG, HALF1_LAG = 1, 2, 3, 5, 7
        ATT_T_LAG, ATT_LO_LAG, OPROJ_LAG, X1_LAG, SQUARES_LAG, POW_LAG = 8, 8, 9, 9, 10, 10
        NORM2_LAG, X2T_LAG, X2T_OUT_LAG = 11, 11, 11
        ROUTER_SLOT = NG + 2
        QUARTER = NTOK // 4
        FILL_TAIL, FILL_MOE = 12, 10
        TAIL = X2T_OUT_LAG - GPB + 1
        PREFETCHES = 16 * (HPC + 1)

        def due(i, s, lag, step=1, last=NG):
            n = s - lag
            if n % step:
                return False
            return not isinstance(i, int) or 0 <= SLOTS * i + n < last

        def last_lag(lag, i, s):
            early = isinstance(i, int) and i > 0 and s >= (4 if lag == X2T_LAG else 3)
            return lag - 1 if early else lag

        def schedule(eng, body, iterations, tail):
            body(0, range(SLOTS))
            with eng.Fori(1, iterations) as i:
                body(i, range(SLOTS))
            body(iterations, range(tail))

        X_LAG, GU_LAG, H_LAG, Y_LAG, SEND_LAG, FREE_LAG = 0, 1, 2, 3, 7, 9

        def tile_due(i, s, lag):
            return not isinstance(i, int) or 1 <= SLOTS * i + s - lag <= NTILES

        def tile_past(i, s, lag, back):
            return not isinstance(i, int) or SLOTS * i + s - lag > back

        FINAL = [range(0, NB // 2 - 1), range(NB // 2 - 1, NB - 2), range(NB - 2, NB)]
        HALF = NTOK // 2
        JOBS = []
        for hf in range(2):
            keys = [("k", mc, hf) for mc in range(KC)]
            turns = [("t", 2 * hf, 0), ("t", 2 * hf + 1, 0)]
            values = [("v", 2 * hf, 0), ("v", 2 * hf + 1, 0)]
            JOBS += (keys + turns + values if hf == 0 else turns + values + keys) + [("q", mc, hf) for mc in range(KC)]

        def job(kind, a, hf=0):
            return JOBS.index((kind, a, hf)) + 1

        block = ctx.enter_context(nc.Block())

        @block.sync
        def _(sp):
            sp.dma_start(xs[:, 0:NB // 2, :], x_v[:, 0:NB // 2, :]).then_inc(in_x[0], 16)
            for half in range(2):
                sp.dma_start(rawkv[L * half:L * half + L, :], WkvT).then_inc(in_kv, 16)
            for half in range(2):
                sp.dma_start(rawc[L * half:L * half + L, :], ctxT).then_inc(in_c, 16)
            sp.dma_start(xs[:, NB // 2:NB, :], x_v[:, NB // 2:NB, :]).then_inc(in_x[1], 16)
            sp.dma_start(cst[:, :], consts).then_inc(in_const, 16)
            sp.dma_start(cst16[:, :], consts16).then_inc(in_const, 16)
            sp.dma_start(rawq, WqT.rearrange("(c p) n -> p c n", p=P)).then_inc(in_q, 16)
            sp.dma_start(gate[:, 0:1], g_attn.partition_broadcast(P)).then_inc(in_g, 16)
            sp.dma_start(gate[:, 1:2], g_ffn.partition_broadcast(P)).then_inc(in_g, 16)
            sp.dma_start(rawo, WoT.rearrange("(c p) n -> p c n", p=P)).then_inc(in_o, 16)
            sp.dma_start(wrr[:, :, :], Wr.rearrange("(c p) n -> p c n", p=P)).then_inc(in_o, 16)

            def load_keys(u, b):
                for j in range(HPC):
                    rows = slice(HD * j, HD * j + HD)
                    sp.dma_start(f(kbd[rows, u, :, j, :]), f(kT[rows, :, bass.ts(b, P)])).then_inc(kq_loaded[u], 16)

            def load_queries(u, b):
                sp.dma_start(f(qb[:, u, :, :]), f(qT[:, :, bass.ts(b, P)])).then_inc(kq_loaded[u], 16)

            def prefetch(u, b):
                load_keys(u, b)
                load_queries(u, b)

            def load_expert(e, slot):
                sp.dma_start(stage[:, slot, 0:KC * F2].rearrange("p (c n) -> p c n", c=KC),
                             Wgu[e].rearrange("(c p) n -> p c n", p=P)).then_inc(in_w[slot], 16)
                sp.dma_start(stage[:, slot, KC * F2:].rearrange("p (c n) -> p c n", c=KC),
                             Wd[e].rearrange("(c p) n -> p c n", p=P)).then_inc(in_w[slot], 16)

            sp.wait_ge(job_hi, job("k", KC - 1, 0))
            sp.wait_ge(job_lo, job("k", KC - 1, 0))
            for u in range(2):
                sp.wait_ge(kbd_zeroed[u], 1)
                load_keys(u, u)
                if u == 0:
                    sp.wait_ge(job_hi, job("q", KC - 1, 0))
                    sp.wait_ge(job_lo, job("q", KC - 1, 0))
                load_queries(u, u)
            sp.wait_ge(wq_split, 1)
            sp.wait_ge(wkv_split, 1)
            sp.wait_ge(wo_split, 1)
            sp.wait_ge(job_lo, len(JOBS))

            def store(b, u):
                sp.wait_ge(norm2, b + 1)
                sp.dma_start(xnd[bass.ds(b * P, P), :], nrm[:, u, :]).then_inc(xn_stored[u], 16)
                sp.dma_start(xs[:, bass.ds(b, 1), :].rearrange("p b d -> p (b d)"), nrm[:, 2 + u, :]
                             ).then_inc(xn_stored[u], 16)

            def feed(i):
                if not isinstance(i, int) or i > 1:
                    store(2 * i - 4, 0)
                sp.wait_ge(scores_done, SLOTS * i - GPB)
                prefetch(0, 2 * i)
                if not isinstance(i, int) or i > 1:
                    sp.wait_ge(w_split, PIECES * (2 * i - 3))
                load_expert(2 * i - 2, 0)
                if not isinstance(i, int) or i > 1:
                    store(2 * i - 3, 1)
                sp.wait_ge(scores_done, SLOTS * i)
                prefetch(1, 2 * i + 1)
                if not isinstance(i, int) or i > 1:
                    sp.wait_ge(w_split, PIECES * (2 * i - 2))
                load_expert(2 * i - 1, 1)
            feed(1)
            with sp.Fori(2, NB // 2) as i:
                feed(i)
            for e in range(E - 2, E):
                store(NB - 4 + e % 2, e % 2)
                sp.wait_ge(w_split, PIECES * (e - 1))
                load_expert(e, e % 2)
            for b in range(NB - 2, NB):
                store(b, b % 2)

            for s in range(SLOTS):
                sp.wait_ge(y_sent[s], 16 * (ROUNDS if s > 0 else ROUNDS - 1))
            yout_v = yout[0:TOPK * NTOK, :].rearrange("(k b p) d -> k p b d", k=TOPK, p=P)
            for q, tiles in enumerate(FINAL):
                part = slice(tiles.start, tiles.stop)
                for k in range(TOPK):
                    sp.dma_start(yk[:, k, part, :], yout_v[k, :, part, :]).then_inc(yk_in[k][q], 16)
            for q, tiles in enumerate(FINAL):
                for t in tiles:
                    if t < tiles[-1]:
                        sp.wait_ge(add1_done, t - q + 1)
                    else:
                        sp.wait_ge(last_done, q + 1)
                    sp.dma_start(out_v[:, t, :], xs[:, t, :]).then_inc(out_done, 16)
            sp.wait_ge(out_done, 16 * NB)

        @block.gpsimd
        def _(pool):
            nc.gpsimd.memset(mhalf[:, :, :], -0.5).then_inc(mhalf_set, 1)
            nc.gpsimd.memset(one[:, :], 1.0).then_inc(mhalf_set, 1)
            for n, (started, events) in enumerate(
                    [(counter, 1) for counter in (oproj_done, x1_done, x2T_done, x2T_lo)]
                    + [(counter, 32) for counter in xn_stored] + [(ys_free, SLOTS)]):
                nc.gpsimd.memset(unused[:, n:n + 1], 0.0).then_inc(started, events)
            for half in range(2):
                t = bass.ts(half, NB // 2)
                pool.wait_ge(eps1, half + 1)
                if half == 0:
                    pool.wait_ge(mhalf_set, 2)
                nc.gpsimd.tensor_tensor(rstd[:, t, :], mv[:, t, 1:2], mhalf[:, t, :], ALU.pow).then_inc(rstd1, 1)
                if half == 0:
                    for hf in range(2):
                        tok = bass.ts(hf, HALF)
                        pool.wait_ge(c_hi, hf + 1)
                        nc.gpsimd.tensor_tensor(cT[:, 1, tok], rawc[:, tok], f(cT[:, 0, tok]), ALU.subtract).then_inc(c_split, 1)
            pool.wait_ge(wq_hi, 1)
            nc.gpsimd.tensor_tensor(wq[:, 1], rawq, f(wq[:, 0]), ALU.subtract).then_inc(wq_split, 1)
            nc.gpsimd.memset(vx[:, :, :, 3 * HD:VW], 1.0).then_inc(ones_set, 1)
            nc.gpsimd.memset(f(kbd[:, 1, :, :, :]), 0.0).then_inc(kbd_zeroed[1], 1)
            for pair in range(NB // 2):
                if pair == 2:
                    pool.wait_ge(wo_hi, 1)
                    nc.gpsimd.tensor_tensor(wo[:, 1], rawo, f(wo[:, 0]), ALU.subtract).then_inc(wo_split, 1)
                pool.wait_ge(v2_done, pair + 1)
                r = vres[:, pair % 2, :].rearrange("p (g d) -> p g d", d=HD)
                v = vx[:, 2 * pair:2 * pair + 2, :, :].rearrange("p b h w -> p (b h) w")
                nc.gpsimd.tensor_tensor(v[:, :, 2 * HD:3 * HD], r, v[:, :, HD:2 * HD],
                                        ALU.subtract).then_inc(v3_done, 1)
            pool.wait_ge(wr_hi, 1)
            nc.gpsimd.tensor_tensor(wr[:, 1], wrr[:, :, :], f(wr[:, 0]), ALU.subtract).then_inc(wr_split, 1)

            def split_piece(e, n, slot, count):
                part = slice(PIECE * n, PIECE * n + PIECE)
                src = stage[:, slot, part]
                hi = W[:, bass.ds(e, 1), 0, part].rearrange("p e w -> p (e w)")
                lo = W[:, bass.ds(e, 1), 1, part].rearrange("p e w -> p (e w)")
                nc.gpsimd.tensor_tensor(hi, src, one[:, :].to_broadcast([P, PIECE]), ALU.mult).then_inc(w_hi, 1)
                pool.wait_ge(w_hi, count)
                nc.gpsimd.tensor_tensor(lo, src, f(hi), ALU.subtract).then_inc(w_split, 1)

            PIECE_SLOTS = {2: (0,), 3: (1,), 4: (2,), 6: (3,), 7: (4, 5)}

            def body(i, slots):
                for s in slots:
                    if due(i, s, last_lag(POW_LAG, i, s), GPB):
                        n = (s - last_lag(POW_LAG, i, s)) // GPB
                        u = n % 2
                        b = 2 * i + n
                        pool.wait_ge(squares2, b + 1)
                        nc.gpsimd.tensor_tensor(mv2[:, u, 1:2], mv2[:, u, 1:2], d_eps, ALU.add).then_inc(eps2, 1)
                        pool.wait_ge(eps2, b + 1)
                        nc.gpsimd.tensor_tensor(mv2[:, u, 1:2], mv2[:, u, 1:2], mhalf[:, 0, :], ALU.pow).then_inc(rsum2, 1)
                        pool.wait_ge(rsum2, b + 1)
                        nc.gpsimd.tensor_tensor(rstd2[:, u, :], mv2[:, u, 1:2], root_d, ALU.mult).then_inc(rstd2_done, 1)
                    for n in PIECE_SLOTS.get(s, ()):
                        half = n // PIECES
                        if isinstance(i, int):
                            continue
                        e = 2 * i - 2 + half
                        if n % PIECES == 0:
                            pool.wait_ge(in_w[half], 32 * i)
                        if n == PIECES:
                            for u in range(2):
                                pool.wait_ge(kq_loaded[u], PREFETCHES * (i + 1))
                        split_piece(e, n % PIECES, half, PIECES * e + n % PIECES + 1)
            schedule(pool, body, NB // 2, TAIL)
            for e in range(E - 2, E):
                pool.wait_ge(in_w[e % 2], 32 * (NB // 2))
                for n in range(PIECES):
                    split_piece(e, n, e % 2, PIECES * e + n + 1)
            pool.wait_ge(idx_set, 1)
            for u in range(2):
                pool.wait_ge(xn_stored[u], 32 + 32 * NB // 2)

            def moe(i, slots):
                for s in slots:
                    sent = SLOTS * i + s - FREE_LAG
                    if 1 <= sent <= NTILES - SLOTS:
                        pool.wait_ge(y_sent[sent % SLOTS], 16 * -(-sent // SLOTS))
                        nc.gpsimd.memset(unused[:, 6 + sent:7 + sent], 0.0).then_inc(ys_free, 1)
                    if tile_due(i, s, 0):
                        if tile_past(i, s, 0, SLOTS):
                            pool.wait_ge(xgT_done, SLOTS * i + s - SLOTS)
                        nc.gpsimd.indirect_dma_start(xg[:, s, :], None, xnd,
                                                     bass.IndirectOffsetOnAxis(ap=idx[:, 0, SLOTS * i + s:SLOTS * i + s + 1], axis=0)
                                                     ).then_inc(xg_in[s], 16)
                    if tile_due(i, s, SEND_LAG):
                        n = (s - SEND_LAG) % SLOTS
                        if SLOTS * i + s - SEND_LAG == 1:
                            pool.wait_ge(idx_set, 2)
                        pool.wait_ge(y_out, SLOTS * i + s - SEND_LAG)
                        j = SLOTS * i + s - SEND_LAG
                        nc.gpsimd.indirect_dma_start(yout, bass.IndirectOffsetOnAxis(ap=idx[:, 1, j:j + 1], axis=0),
                                                     ys[:, n, :], None).then_inc(y_sent[n], 16)
            for i in range(ROUNDS):
                moe(i, range(SLOTS))
            moe(ROUNDS, range(SEND_LAG))
            for q, tiles in enumerate(FINAL):
                t = tiles[-1]
                pool.wait_ge(add0_done, t + 1)
                pool.wait_ge(weighted, q + 1)
                nc.gpsimd.tensor_tensor(xs[:, t, :], xs[:, t, :], ys[:, t, :], ALU.add).then_inc(last_done, 1)

        @block.scalar
        def _(act):
            act.wait_ge(in_kv, 32)
            nc.scalar.copy(wkv, rawkv).then_inc(wkv_hi, 1)
            act.wait_ge(in_c, 32)
            for hf in range(2):
                nc.scalar.copy(cT[:, 0, bass.ts(hf, HALF)], rawc[:, bass.ts(hf, HALF)]).then_inc(c_hi, 1)
            act.wait_ge(in_q, 16)
            nc.scalar.copy(wq[:, 0], rawq).then_inc(wq_hi, 1)

            def second_part(pair):
                act.wait_ge(job_lo, job("v", pair))
                v = vx[:, 2 * pair:2 * pair + 2, :, :].rearrange("p b h w -> p (b h) w")
                nc.scalar.copy(v[:, :, HD:2 * HD], vres[:, pair % 2, :].rearrange("p (g d) -> p g d", d=HD)
                               ).then_inc(v2_done, 1)
            for n, (kind, a, hf) in enumerate(JOBS):
                bank = ps[:, n % 8, :]
                act.wait_ge(job_done, n + 1)
                if kind == "k":
                    op = nc.scalar.copy(kT[:, a, bass.ts(hf, HALF)], bank)
                elif kind == "q":
                    op = nc.scalar.activation(qT[:, a, bass.ts(hf, HALF)], bank, ACT.Copy, scale=QSCALE)
                elif kind == "t":
                    op = nc.scalar.copy(xT[:, 0, :, bass.ts(a, 2 * P)], bank.rearrange("p (c t) -> p c t", c=KC))
                else:
                    v = vx[:, 2 * a:2 * a + 2, :, :].rearrange("p b h w -> p (b h) w")
                    op = nc.scalar.copy(v[:, :, 0:HD], bank.rearrange("p (g d) -> p g d", d=HD))
                op.then_inc(job_hi, 1)
                for pair in range(NB // 2):
                    if n == job("v", pair):
                        second_part(pair)
                if n == job("v", 1) + 1:
                    act.wait_ge(in_o, 32)
                    nc.scalar.copy(wo[:, 0], rawo).then_inc(wo_hi, 1)
                    nc.scalar.copy(wr[:, 0], wrr[:, :, :]).then_inc(wr_hi, 1)
            act.wait_ge(in_g, 32)
            nc.scalar.activation(tg[:, :], gate[:, :], ACT.Tanh).then_inc(tg_set, 1)

            def body(i, slots):
                for s in slots:
                    if due(i, s, EVICT_LAG):
                        n = s - EVICT_LAG
                        act.wait_ge(turned, SLOTS * i + n + 1)
                        if not isinstance(i, int) or SLOTS * i + n >= 2:
                            act.wait_ge(pv_done, SLOTS * i + n - 1)
                        nc.scalar.activation(pth[:, n % 2, :], ps[:, 2 + n % 2, :], ACT.Copy,
                                             scale=PSCALE).then_inc(pth_done, 1)
                    if due(i, s, last_lag(SQUARES_LAG, i, s), GPB):
                        n = (s - last_lag(SQUARES_LAG, i, s)) // GPB
                        act.wait_ge(mean2, 2 * i + n + 1)
                        nc.scalar.activation(junk[:, :], nrm[:, 2 + n % 2, :], ACT.Square, bias=nm2[:, n % 2, :],
                                             accum_out=mv2[:, n % 2, 1:2]).then_inc(squares2, 1)
                    if due(i, s, last_lag(ATT_LO_LAG, i, s), GPB):
                        n = (s - last_lag(ATT_LO_LAG, i, s)) // GPB
                        act.wait_ge(attT_done, 2 * i + n + 1)
                        if not isinstance(i, int) or 2 * i + n >= 1:
                            act.wait_ge(oproj_done, 2 * i + n + 1)
                        nc.scalar.copy(rT[:, 0, 0], ps[:, 6, 0:KC * P].rearrange("p (c t) -> p c t", c=KC)
                                       ).then_inc(attT_hi, 1)
                    if due(i, s, 0):
                        act.wait_ge(negm_done, SLOTS * i + s + 1)
                        if not isinstance(i, int) or i > 0 or s >= 2:
                            act.wait_ge(turned, SLOTS * i + s - 1)
                        else:
                            act.wait_ge(v3_done, NB // 2)
                        for j in range(GH):
                            op = nc.scalar.activation(prob[:, s % 2, j * P:(j + 1) * P],
                                                      ps[:, s % 2, j * P:(j + 1) * P], ACT.Exp,
                                                      bias=negm[:, s % 2, j:j + 1])
                        op.then_inc(exp_done, 1)
                    if due(i, s, last_lag(X2T_OUT_LAG, i, s), GPB):
                        n = (s - last_lag(X2T_OUT_LAG, i, s)) // GPB
                        act.wait_ge(x2T_done, 2 * i + n + 2)
                        nc.scalar.copy(xT[:, 0, :, bass.ts(2 * i + n, P)],
                                       ps[:, 6, 0:KC * P].rearrange("p (c t) -> p c t", c=KC)).then_inc(x2T_hi, 1)
            schedule(act, body, NB // 2, TAIL)

            for hf in range(2):
                act.wait_ge(rt_done, hf + 1)
                nc.scalar.copy(lgT[:, bass.ts(hf, HALF)], ps[0:E, hf, :]).then_inc(rt_out, 1)
            act.wait_ge(rt_exp_in, 1)
            nc.scalar.activation(pr[:, :, :], lg[:, :, :], ACT.Exp).then_inc(rt_exp, 1)
            nc.scalar.activation(junk[:, 0:1], gate[:, 0:1], ACT.Silu)
            act.wait_ge(place_set, 1)
            for m in range(NB, TOPK * NB):
                nc.scalar.activation(at_place[:, m, :], col_no, ACT.Abs, scale=-1.0, bias=place[:, m:m + 1]
                                     ).then_inc(distance_set, 1)
            act.wait_ge(distance_set, NB)
            nc.scalar.activation(at_place[:, NB:, :], at_place[:, NB:, :], ACT.Relu, scale=-1.0, bias=one[:, :]
                                 ).then_inc(sorted_in, 1)

            def moe(i, slots):
                for s in slots:
                    if tile_due(i, s, X_LAG):
                        act.wait_ge(xgT_done, SLOTS * i + s)
                        if tile_past(i, s, X_LAG, 2):
                            act.wait_ge(gu_done, SLOTS * i + s - 2)
                        nc.scalar.copy(xT[:, 0, :, bass.ts(s % 2, P)], ps[:, s % 2, 0:D].rearrange("p (c t) -> p c t", c=KC)
                                       ).then_inc(xgT_hi, 1)
                    if tile_due(i, s, GU_LAG):
                        n = (s - GU_LAG) % 2
                        act.wait_ge(gu_done, SLOTS * i + s - GU_LAG)
                        if tile_past(i, s, GU_LAG, 2):
                            act.wait_ge(h_done, SLOTS * i + s - GU_LAG - 2)
                        nc.scalar.activation(sg[:, n, 0:D], ps[:, 2 + n, 0:D], ACT.Silu).then_inc(silu_done, 1)
                    if tile_due(i, s, H_LAG):
                        n = (s - H_LAG) % 2
                        act.wait_ge(hT_done, SLOTS * i + s - H_LAG)
                        if tile_past(i, s, H_LAG, 2):
                            act.wait_ge(y_done, SLOTS * i + s - H_LAG - 2)
                        nc.scalar.copy(rT[:, n, 0], ps[:, 4 + n, 0:D].rearrange("p (c t) -> p c t", c=KC)
                                       ).then_inc(hT_hi, 1)
                    if tile_due(i, s, Y_LAG):
                        n = (s - Y_LAG) % SLOTS
                        act.wait_ge(y_done, SLOTS * i + s - Y_LAG)
                        act.wait_ge(ys_free, SLOTS * i + s - Y_LAG)
                        nc.scalar.copy(ys[:, n, :], ps[:, 6 + n % 2, 0:D]).then_inc(y_out, 1)
            schedule(act, moe, ROUNDS, Y_LAG)
            for q, tiles in enumerate(FINAL):
                t = tiles[-1]
                act.wait_ge(yk_in[1][q], 16)
                nc.scalar.activation(ys[:, t, :], yk[:, 1, t, :], ACT.Copy, scale=wk[:, 1, t:t + 1]).then_inc(weighted, 1)

        @block.vector
        def _(dve):
            nc.vector.memset(f(kbd[:, 0, :, :, :]), 0.0).then_inc(kbd_zeroed[0], 1)
            def statistics(half):
                dve.wait_ge(in_x[half], 16)
                first = half * NB // 2
                for b in range(first, first + NB // 2):
                    nc.vector.bn_stats(stat[:, b, :], xs[:, b, :]).then_inc(stats1, 1)
                for b in range(first, first + NB // 2):
                    dve.wait_ge(stats1, b + 1)
                    nc.vector.bn_aggr(mv[:, b, :], stat[:, b, :]).then_inc(aggr1, 1)
                dve.wait_ge(aggr1, first + NB // 2)
                t = bass.ts(half, NB // 2)
                nc.vector.tensor_scalar(mv[:, t, 1:2], mv[:, t, 1:2], EPS, None, ALU.add).then_inc(eps1, 1)

            def normalise(half):
                dve.wait_ge(rstd1, half + 1)
                for b in range(half * NB // 2, (half + 1) * NB // 2):
                    if b >= 4:
                        dve.wait_ge(job_done, job("t", b // 2 - 2))
                    nc.vector.tensor_scalar(nrm[:, b % 4, :], xs[:, b, :], mv[:, b, 0:1], rstd[:, b, :],
                                            ALU.subtract, ALU.mult).then_inc(norm1, 1)

            statistics(0)
            dve.wait_ge(wkv_hi, 1)
            nc.vector.tensor_tensor(wkv[L:P, :], rawkv[L:P, :], f(wkv[L:P, :]), ALU.subtract).then_inc(wkv_split, 1)
            normalise(0)
            statistics(1)

            def job_low(n):
                kind, a, hf = JOBS[n]
                bank = ps[:, n % 8, :]
                dve.wait_ge(job_hi, n + 1)
                if kind == "k":
                    half = bass.ts(hf, HALF)
                    op = nc.vector.tensor_tensor(kT[:, KC + a, half], bank, f(kT[:, a, half]), ALU.subtract)
                elif kind == "q":
                    half = bass.ts(hf, HALF)
                    op = nc.vector.scalar_tensor_tensor(qT[:, KC + a, half], bank, QSCALE, f(qT[:, a, half]),
                                                        ALU.mult, ALU.subtract)
                elif kind == "t":
                    op = nc.vector.tensor_tensor(xT[:, 1, :, bass.ts(a, 2 * P)], bank.rearrange("p (c t) -> p c t", c=KC),
                                                 f(xT[:, 0, :, bass.ts(a, 2 * P)]), ALU.subtract)
                else:
                    if a >= 2:
                        dve.wait_ge(v3_done, a - 1)
                    v = vx[:, 2 * a:2 * a + 2, :, :].rearrange("p b h w -> p (b h) w")
                    op = nc.vector.tensor_tensor(vres[:, a % 2, :].rearrange("p (g d) -> p g d", d=HD),
                                                 bank.rearrange("p (g d) -> p g d", d=HD), v[:, :, 0:HD], ALU.subtract)
                op.then_inc(job_lo, 1)

            for n in range(len(JOBS)):
                if n == job("q", 0, 0) - 1:
                    normalise(1)
                job_low(n)

            def normalise2(i, s):
                if due(i, s, last_lag(NORM2_LAG, i, s), GPB):
                    n = (s - last_lag(NORM2_LAG, i, s)) // GPB
                    b, u = 2 * i + n, n % 2
                    dve.wait_ge(rstd2_done, b + 1)
                    if not isinstance(i, int) or b >= 2:
                        dve.wait_ge(x2T_done, b + 1)
                    nc.vector.tensor_scalar(nrm[:, u, :], nrm[:, 2 + u, :], nm2[:, u, :], rstd2[:, u, :],
                                            ALU.add, ALU.mult).then_inc(norm2, 1)

            def body(i, slots):
                for s in slots:
                    if due(i, s, 0):
                        dve.wait_ge(scores_done, SLOTS * i + s + 1)
                        if not isinstance(i, int) or i > 0 or s >= 2:
                            dve.wait_ge(exp_done, SLOTS * i + s - 1)
                        nc.vector.tensor_reduce(negm[:, s % 2, :], ps[:, s % 2, :].rearrange("p (h k) -> p h k", h=GH),
                                                AX_X, ALU.max, negate=True).then_inc(negm_done, 1)
                    if not isinstance(i, int):
                        normalise2(i, s)
                    if due(i, s, EVICT_LAG):
                        n = s - EVICT_LAG
                        dve.wait_ge(pth_done, SLOTS * i + n + 1)
                        if not isinstance(i, int) or SLOTS * i + n >= 2:
                            dve.wait_ge(pv_done, SLOTS * i + n - 1)
                        nc.vector.scalar_tensor_tensor(ptl[:, n % 2, :], ps[:, 2 + n % 2, :], PSCALE,
                                                       pth[:, n % 2, :], ALU.mult, ALU.subtract).then_inc(ptl_done, 1)
                    for part, lag in ((0, HALF0_LAG), (1, HALF1_LAG)):
                        if due(i, s, lag, GPB):
                            n = (s - lag) // GPB
                            half = 2 * (2 * i + n) + part
                            bank = ps[:, 4 + part, :].rearrange("p (h w) -> p h w", w=64)
                            o = slice(P * part, P * part + P)
                            dve.wait_ge(pv_done, GPB * (2 * i + n) + 2 * part + 2)
                            nc.vector.tensor_reduce(attr[:, o].rearrange("p (h d) -> p h d", d=HD),
                                                    bank[:, :, 0:3 * HD].rearrange("p h (c d) -> p h d c", c=3),
                                                    AX_X, ALU.add).then_inc(sums_done, 1)
                            nc.vector.reciprocal(rinv[:, :].unsqueeze(2),
                                                 bank[:, :, 3 * HD:3 * HD + 1]).then_inc(sums_done, 1)
                            dve.wait_ge(sums_done, 2 * half + 2)
                            if not isinstance(i, int) or 2 * i + n >= 1:
                                dve.wait_ge(attT_done, 2 * i + n)
                            nc.vector.tensor_tensor(att[:, o].rearrange("p (h d) -> p h d", d=HD),
                                                    attr[:, o].rearrange("p (h d) -> p h d", d=HD),
                                                    rinv[:, :].unsqueeze(2).to_broadcast([P, HPC, HD]),
                                                    ALU.mult).then_inc(att_done, 1)
                    if isinstance(i, int):
                        normalise2(i, s)
                    if due(i, s, last_lag(ATT_LO_LAG, i, s), GPB):
                        n = (s - last_lag(ATT_LO_LAG, i, s)) // GPB
                        dve.wait_ge(attT_hi, 2 * i + n + 1)
                        if not isinstance(i, int) or 2 * i + n >= 1:
                            dve.wait_ge(oproj_done, 2 * i + n + 1)
                        nc.vector.tensor_tensor(rT[:, 0, 1], ps[:, 6, 0:KC * P].rearrange("p (c t) -> p c t", c=KC),
                                                f(rT[:, 0, 0]), ALU.subtract).then_inc(attT_lo, 1)
                    if due(i, s, last_lag(X1_LAG, i, s), GPB):
                        n = (s - last_lag(X1_LAG, i, s)) // GPB
                        b, u = 2 * i + n, n % 2
                        xb = xs[:, bass.ds(b, 1), :].rearrange("p b d -> p (b d)")
                        dve.wait_ge(oproj_done, b + 2)
                        if isinstance(i, int) and 2 * i + n == 0:
                            dve.wait_ge(tg_set, 1)
                        if not isinstance(i, int) or b >= 2:
                            dve.wait_ge(xn_stored[u], 32 + 32 * (i + n // 2))
                        nc.vector.scalar_tensor_tensor(nrm[:, 2 + u, :], ps[:, 7, 0:D], tg[:, 0:1], xb, ALU.mult, ALU.add,
                                                       accum_out=mv2[:, u, 0:1]).then_inc(x1_done, 1)
                        dve.wait_ge(x1_done, b + 2)
                        nc.vector.tensor_scalar(nm2[:, u, :], mv2[:, u, 0:1], -1.0 / D, None, ALU.mult).then_inc(mean2, 1)
                    if due(i, s, last_lag(X2T_OUT_LAG, i, s), GPB):
                        n = (s - last_lag(X2T_OUT_LAG, i, s)) // GPB
                        b = 2 * i + n
                        dve.wait_ge(x2T_hi, b + 1)
                        nc.vector.tensor_tensor(xT[:, 1, :, bass.ts(b, P)],
                                                ps[:, 6, 0:KC * P].rearrange("p (c t) -> p c t", c=KC),
                                                f(xT[:, 0, :, bass.ts(b, P)]), ALU.subtract).then_inc(x2T_lo, 1)
            schedule(dve, body, NB // 2, TAIL)

            steps = [0]

            def step(ins, running=0):
                steps[0] += 1
                ins.then_inc(rt_step, 1)
                dve.wait_ge(rt_step, steps[0] - running)

            def over_e(ap):
                return ap.unsqueeze(2).to_broadcast([P, NB, E])

            dve.wait_ge(rt_T, 1)
            logits = ps[:, 2, 0:NB * E].rearrange("p (t e) -> p t e", e=E)
            step(nc.vector.tensor_reduce(lmax[:, :], logits, AX_X, ALU.max))
            nc.vector.tensor_tensor(lg[:, :, :], logits, over_e(lmax[:, :]), ALU.subtract).then_inc(rt_exp_in, 1)
            dve.wait_ge(rt_exp, 1)
            step(nc.vector.tensor_reduce(psum_r[:, :], pr[:, :, :], AX_X, ALU.add))
            step(nc.vector.reciprocal(wk[:, 0], psum_r[:, :]))
            step(nc.vector.tensor_tensor(pr[:, :, :], pr[:, :, :], over_e(wk[:, 0]), ALU.mult))
            for k in range(TOPK):
                if k > 0:
                    step(nc.vector.scalar_tensor_tensor(pr[:, :, :], choice[:, 0], -4.0, pr[:, :, :], ALU.mult, ALU.add))
                    step(nc.vector.tensor_reduce(wk[:, k], pr[:, :, :], AX_X, ALU.max))
                step(nc.vector.tensor_tensor(order[:, :, :], pr[:, :, :], over_e(wk[:, k]), ALU.is_equal))
                step(nc.vector.tensor_tensor(order[:, :, :], order[:, :, :], falling.unsqueeze(1).to_broadcast([P, NB, E]),
                                             ALU.mult))
                step(nc.vector.tensor_reduce(lmax[:, :], order[:, :, :], AX_X, ALU.max))
                step(nc.vector.tensor_tensor(choice[:, k], order[:, :, :], over_e(lmax[:, :]), ALU.is_equal))
            nc.vector.tensor_tensor(chosen[:, :, :], choice[:, 0], choice[:, 1], ALU.add).then_inc(chosen_set, 1)
            step(nc.vector.tensor_tensor(psum_r[:, :], wk[:, 0], wk[:, 1], ALU.add))
            step(nc.vector.reciprocal(psum_r[:, :], psum_r[:, :]))
            step(nc.vector.tensor_scalar(psum_r[:, :], psum_r[:, :], tg[:, 1:2], None, ALU.mult))
            step(nc.vector.tensor_tensor(wk, wk, psum_r[:, :].unsqueeze(1).to_broadcast([P, TOPK, NB]), ALU.mult))

            def over_k(ap):
                return ap.unsqueeze(1).to_broadcast([P, TOPK, NB, E])
            dve.wait_ge(counted, 1)
            count = ps[:, 3, NB * E:NB * E + E].unsqueeze(2).to_broadcast([P, E, NB])
            step(nc.vector.tensor_tensor(picked, choice, over_k(ps[:, 3, 0:NB * E].rearrange("p (t e) -> p t e", e=E)),
                                         ALU.mult), 1)
            step(nc.vector.tensor_tensor(full, count, fulls, ALU.is_gt), 1)
            step(nc.vector.tensor_reduce(rank_k.rearrange("p (k t) -> p k t", k=TOPK), picked, AX_X, ALU.add), 1)
            step(nc.vector.tensor_reduce(ntiles, full, AX_X, ALU.add), 1)
            step(nc.vector.tensor_scalar(over, rank_k, -(P - 1) / 2, 1.0 / P, ALU.add, ALU.mult), 1)
            step(nc.vector.tensor_tensor(cum, ntiles.unsqueeze(1).to_broadcast([P, E, E]), upto, ALU.mult), 1)
            step(nc.vector.tensor_scalar(over, over, ROUND, None, ALU.add), 1)
            step(nc.vector.tensor_reduce(cum_end, cum, AX_X, ALU.add), 1)
            step(nc.vector.tensor_scalar(nfull, over, -ROUND, None, ALU.add), 1)
            step(nc.vector.tensor_tensor(cum_start, cum_end, ntiles, ALU.subtract), 1)
            nc.vector.scalar_tensor_tensor(place, nfull, -float(P), rank_k, ALU.mult, ALU.add).then_inc(place_set, 1)
            dve.wait_ge(place_set, 1)
            nc.vector.tensor_tensor(at_place[:, 0:NB, :], place[:, 0:NB].unsqueeze(2).to_broadcast([P, NB, P]),
                                    col_no.unsqueeze(1).to_broadcast([P, NB, P]), ALU.is_equal
                                    ).then_inc(sorted_in, 1)
            dve.wait_ge(rt_step, steps[0])
            step(nc.vector.tensor_tensor(picked.rearrange("p k t e -> p (k t) e"), choice.rearrange("p k t e -> p (k t) e"),
                                         cum_start.unsqueeze(1).to_broadcast([P, TOPK * NB, E]), ALU.mult))
            step(nc.vector.tensor_reduce(tile_k.rearrange("p (k t) -> p k t", k=TOPK), picked, AX_X, ALU.add))
            step(nc.vector.tensor_tensor(tile_k, tile_k, nfull, ALU.add))
            step(nc.vector.tensor_tensor(in_tile, tile_k.unsqueeze(2).to_broadcast([P, TOPK * NB, J]),
                                         tile_no.unsqueeze(1).to_broadcast([P, TOPK * NB, J]), ALU.is_equal))
            nc.vector.tensor_scalar(at_tile[:, :, 0, :], in_tile, part_no, None, ALU.mult).then_inc(sorted_in, 1)
            nc.vector.tensor_tensor(at_tile[:, :, 1, :], in_tile, block_no.unsqueeze(2).to_broadcast([P, TOPK * NB, J]),
                                    ALU.mult).then_inc(sorted_in, 1)
            step(nc.vector.tensor_tensor(past, cum_end.unsqueeze(1).to_broadcast([P, J, E]),
                                         tile_no.unsqueeze(2).to_broadcast([P, J, E]), ALU.is_le))
            step(nc.vector.tensor_reduce(tile_e, past, AX_X, ALU.add))
            nc.vector.tensor_scalar(tile_expert[:, :], tile_e, float(E - 1), None, ALU.min).then_inc(experts_set, 1)
            dve.wait_ge(sorted_out, 1)
            part, blk = ps[:, 2, 0:J], ps[:, 2, J:2 * J]
            step(nc.vector.tensor_copy(v1, part))
            step(nc.vector.scalar_tensor_tensor(v1, blk, float(P), v1, ALU.mult, ALU.add))
            step(nc.vector.tensor_scalar(c0, v1, float(P + NTOK), -float(NTOK), ALU.is_ge, ALU.mult))
            step(nc.vector.scalar_tensor_tensor(c0, v1, -float(P), c0, ALU.add, ALU.add))
            nc.vector.tensor_scalar(idx[:, 0, :], c0, 0.0, None, ALU.max).then_inc(idx_set, 1)
            step(nc.vector.scalar_tensor_tensor(e0, v1, 0.0, empty_row, ALU.is_equal, ALU.mult))
            nc.vector.scalar_tensor_tensor(idx[:, 1, :], v1, -float(P), e0, ALU.add, ALU.add).then_inc(idx_set, 1)

            def moe(i, slots):
                for s in slots:
                    if tile_due(i, s, X_LAG):
                        dve.wait_ge(xgT_hi, SLOTS * i + s)
                        if tile_past(i, s, X_LAG, 2):
                            dve.wait_ge(gu_done, SLOTS * i + s - 2)
                        nc.vector.tensor_tensor(xT[:, 1, :, bass.ts(s % 2, P)],
                                                ps[:, s % 2, 0:D].rearrange("p (c t) -> p c t", c=KC),
                                                f(xT[:, 0, :, bass.ts(s % 2, P)]), ALU.subtract).then_inc(xgT_lo, 1)
                    if tile_due(i, s, GU_LAG):
                        n = (s - GU_LAG) % 2
                        dve.wait_ge(silu_done, SLOTS * i + s - GU_LAG)
                        if tile_past(i, s, GU_LAG, 2):
                            dve.wait_ge(hT_done, SLOTS * i + s - GU_LAG - 2)
                        nc.vector.tensor_tensor(h[:, n, :], ps[:, 2 + n, D:2 * D], sg[:, n, 0:D],
                                                ALU.mult).then_inc(h_done, 1)
                    if tile_due(i, s, H_LAG):
                        n = (s - H_LAG) % 2
                        dve.wait_ge(hT_hi, SLOTS * i + s - H_LAG)
                        if tile_past(i, s, H_LAG, 2):
                            dve.wait_ge(y_done, SLOTS * i + s - H_LAG - 2)
                        nc.vector.tensor_tensor(rT[:, n, 1], ps[:, 4 + n, 0:D].rearrange("p (c t) -> p c t", c=KC),
                                                f(rT[:, n, 0]), ALU.subtract).then_inc(hT_lo, 1)
            for u in range(2):
                dve.wait_ge(xn_stored[u], 32 + 32 * NB // 2)
            schedule(dve, moe, ROUNDS, H_LAG)

            for q, tiles in enumerate(FINAL):
                for k in range(TOPK):
                    dve.wait_ge(yk_in[k][q], 16)
                    for t in tiles[:len(tiles) - k]:
                        if k == 1:
                            dve.wait_ge(add0_done, t + 1)
                        nc.vector.scalar_tensor_tensor(xs[:, t, :], yk[:, k, t, :], wk[:, k, t:t + 1], xs[:, t, :],
                                                       ALU.mult, ALU.add).then_inc((add0_done, add1_done)[k], 1)

        @block.tensor
        def _(pe):
            def mm3(out_, a_hi, a_lo, b_hi, b_lo, first, last):
                nc.tensor.matmul(out_, a_hi, b_hi, start=first, stop=False)
                nc.tensor.matmul(out_, a_hi, b_lo, start=False, stop=False)
                return nc.tensor.matmul(out_, a_lo, b_hi, start=False, stop=last)

            def keep_clock_up(bank, products):
                for _ in range(products):
                    nc.tensor.matmul(bank, identb, cst16[:, 0:BANK], start=True, stop=True)

            for n, (kind, a, hf) in enumerate(JOBS):
                bank = ps[:, n % 8, :]
                half = bass.ts(hf, HALF)
                if n == 0:
                    pe.wait_ge(wkv_split, 1)
                if kind in "kv":
                    pe.wait_ge(c_split, 2 if (hf if kind == "k" else a >= 2) else 1)
                if n >= 8:
                    pe.wait_ge(job_lo, n - 7)
                if kind == "k":
                    w = wkv[:, a * P:(a + 1) * P]
                    nc.tensor.matmul(bank, w, cT[:, 0, half], start=True, stop=False)
                    mm = nc.tensor.matmul(bank, w, cT[:, 1, half], start=False, stop=True)
                elif kind == "v":
                    for u in range(2):
                        o = bank[:, D * u:D * u + D]
                        tok = bass.ts(2 * a + u, P)
                        nc.tensor.matmul(o, cT[:, 0, tok], wkv[:, D:2 * D], start=True, stop=False)
                        mm = nc.tensor.matmul(o, cT[:, 1, tok], wkv[:, D:2 * D], start=False, stop=True)
                elif kind == "t":
                    pe.wait_ge(in_const, 32)
                    pe.wait_ge(norm1, 2 * a + 2)
                    for u in range(2):
                        for c in range(KC):
                            mm = nc.tensor.transpose(bank[:, 2 * P * c + P * u:2 * P * c + P * u + P],
                                                     nrm[:, (2 * a + u) % 4, c * P:(c + 1) * P], identf)
                else:
                    pe.wait_ge(wq_split, 1)
                    pe.wait_ge(job_lo, job("t", 2 * hf + 1))
                    for c in range(KC):
                        m = slice(a * P, (a + 1) * P)
                        mm = mm3(bank, wq[:, 0, c, m], wq[:, 1, c, m], xT[:, 0, c, half], xT[:, 1, c, half],
                                 c == 0, c == KC - 1)
                mm.then_inc(job_done, 1)

            pe.wait_ge(job_lo, len(JOBS))
            pe.wait_ge(ones_set, 1)
            pe.wait_ge(v3_done, NB // 2)
            pe.wait_ge(wo_split, 1)

            def body(i, slots):
                for s in slots:
                    if due(i, s, 0):
                        u, g = s // GPB, s % GPB
                        c, j0 = g // 2, GH * (g % 2)
                        if g == 0:
                            pe.wait_ge(kq_loaded[u], PREFETCHES * (i + 1))
                        if not isinstance(i, int) or i > 0 or s >= 2:
                            pe.wait_ge(exp_done, SLOTS * i + s - 1)
                        bank = ps[:, s % 2, :]

                        def keys(part):
                            return kbd[:, u, KC * part + c, j0:j0 + GH, :].rearrange("p h k -> p (h k)")
                        nc.tensor.matmul(bank.rearrange("p (h k) -> p h k", h=GH), identb,
                                         mask.unsqueeze(1).to_broadcast([P, GH, P]),
                                         start=True, stop=False)
                        mm3(bank, qb[:, u, c, :], qb[:, u, KC + c, :], keys(0), keys(1), False, True
                            ).then_inc(scores_done, 1)
                    if due(i, s, TURN_LAG):
                        n = s - TURN_LAG
                        pe.wait_ge(exp_done, SLOTS * i + n + 1)
                        if not isinstance(i, int) or SLOTS * i + n >= 2:
                            pe.wait_ge(ptl_done, SLOTS * i + n - 1)
                        for j in range(GH):
                            mm = nc.tensor.transpose(ps[:, 2 + n % 2, j * P:(j + 1) * P],
                                                     prob[:, n % 2, j * P:(j + 1) * P], identf)
                        mm.then_inc(turned, 1)
                    if due(i, s, PV_LAG):
                        n = s - PV_LAG
                        g = n % GPB
                        b = 2 * i + n // GPB
                        pe.wait_ge(ptl_done, SLOTS * i + n + 1)
                        if g % 2 == 0 and (not isinstance(i, int) or 2 * i + n // GPB >= 1):
                            pe.wait_ge(sums_done, 4 * (b - 1) + g + 2)
                        for j in range(GH):
                            hh = GH * (g % 2) + j
                            o = ps[:, 4 + g // 2, 64 * hh:64 * hh + 3 * HD + 1]
                            v = vx[:, bass.ds(b, 1), GH * g + j, 0:3 * HD + 1].rearrange("p b w -> p (b w)")
                            nc.tensor.matmul(o, pth[:, n % 2, j * P:(j + 1) * P], v, start=True, stop=False)
                            mm = nc.tensor.matmul(o, ptl[:, n % 2, j * P:(j + 1) * P], v, start=False, stop=True)
                        mm.then_inc(pv_done, 1)
                    if due(i, s, last_lag(ATT_T_LAG, i, s), GPB):
                        n = (s - last_lag(ATT_T_LAG, i, s)) // GPB
                        b = 2 * i + n
                        pe.wait_ge(att_done, 2 * b + 2)
                        if not isinstance(i, int) or b >= 1:
                            pe.wait_ge(x2T_lo, (NB - 2 if isinstance(i, int) and b == NB - 1 else b) + 1)
                        for c in range(KC):
                            mm = nc.tensor.transpose(ps[:, 6, c * P:(c + 1) * P], att[:, c * P:(c + 1) * P], identf)
                        mm.then_inc(attT_done, 1)
                    if due(i, s, last_lag(OPROJ_LAG, i, s), GPB):
                        n = (s - last_lag(OPROJ_LAG, i, s)) // GPB
                        b = 2 * i + n
                        pe.wait_ge(attT_lo, b + 1)
                        if not isinstance(i, int) or b >= 1:
                            pe.wait_ge(x1_done, b + 1)
                        for c in range(KC):
                            mm = mm3(ps[:, 7, 0:D], rT[:, 0, 0, c, :], rT[:, 0, 1, c, :], wo[:, 0, c, :], wo[:, 1, c, :],
                                     c == 0, c == KC - 1)
                        mm.then_inc(oproj_done, 1)
                        if isinstance(i, int) and b == NB - 1:
                            keep_clock_up(ps[:, 3, :], FILL_TAIL)
                    if due(i, s, last_lag(X2T_LAG, i, s), GPB):
                        n = (s - last_lag(X2T_LAG, i, s)) // GPB
                        b, u = 2 * i + n, n % 2
                        pe.wait_ge(norm2, b + 1)
                        if isinstance(i, int) and i > 0 and b >= NB - 2:
                            pe.wait_ge(attT_lo, NB)
                            pe.wait_ge(x2T_lo, b + 1)
                        else:
                            pe.wait_ge(attT_lo, b + 1)
                        for c in range(KC):
                            mm = nc.tensor.transpose(ps[:, 6, c * P:(c + 1) * P], nrm[:, u, c * P:(c + 1) * P],
                                                     identf)
                        mm.then_inc(x2T_done, 1)
                    if isinstance(i, int) and SLOTS * i + s == ROUTER_SLOT:
                        for q in range(3):
                            router(q)
            def router(q):
                pe.wait_ge(wr_split, 1)
                pe.wait_ge(x2T_lo, 2 * q + 2 + 1)
                tok = bass.ts(q, QUARTER)
                for c in range(KC):
                    mm = mm3(ps[0:E, q // 2, bass.ts(q % 2, QUARTER)], wr[:, 0, c, :], wr[:, 1, c, :],
                             xT[:, 0, c, tok], xT[:, 1, c, tok], c == 0, c == KC - 1)
                if q % 2 == 1:
                    mm.then_inc(rt_done, 1)
            schedule(pe, body, NB // 2, TAIL)
            router(3)

            pe.wait_ge(rt_out, 2)
            for t in range(NB):
                mm = nc.tensor.transpose(ps[:, 2, E * t:E * t + E], lgT[:, t * P:(t + 1) * P], identf[0:E, 0:E])
            mm.then_inc(rt_T, 1)

            pe.wait_ge(chosen_set, 1)
            pe.wait_ge(rt_step, 1)
            nc.tensor.matmul(ps[:, 3, 0:NB * E], before, chosen[:, :, :].rearrange("p t e -> p (t e)"),
                             start=True, stop=False)
            for t in range(NB - 1):
                nc.tensor.matmul(ps[:, 3, (t + 1) * E:NB * E].rearrange("p (t e) -> p t e", e=E), ones,
                                 chosen[:, t:t + 1, :].to_broadcast([P, NB - 1 - t, E]),
                                 start=False, stop=t == NB - 2)
            for t in range(NB):
                mm = nc.tensor.matmul(ps[:, 3, NB * E:NB * E + E], ones, chosen[:, t, :], start=t == 0, stop=t == NB - 1)
            mm.then_inc(counted, 1)

            pe.wait_ge(sorted_in, 4)
            M = TOPK * NB
            for m in range(M):
                mm = nc.tensor.matmul(ps[:, 2, 0:2 * J], at_place[:, m, :], at_tile[:, m, :, :].rearrange("p v j -> p (v j)"),
                                      start=m == 0, stop=m == M - 1)
            mm.then_inc(sorted_out, 1)

            keep_clock_up(ps[:, 4, :], FILL_MOE)
            pe.wait_ge(w_split, PIECES * E)
            pe.wait_ge(experts_set, 1)
            pe.wait_ge(idx_set, 2)

            def tile_experts(i, first, end):
                at = slice(SLOTS * i + first, SLOTS * i + end) if isinstance(i, int) else \
                    bass.ds(SLOTS * i + first, end - first)
                _, values = nc.values_load_multi_w_load_instructions(
                    tile_expert[0:1, at], engines=[mybir.EngineType.PE], min_val=0, max_val=E - 1,
                    skip_runtime_bounds_check_because="the experts are counts from 0, limited to E - 1 where they are written")
                return dict(zip(range(first, end), values))

            def moe(i, slots):
                first, end = -Y_LAG, SLOTS - GU_LAG
                if isinstance(i, int):
                    first, end = max(first, 1 - SLOTS * i), min(end, NTILES + 1 - SLOTS * i)
                experts = tile_experts(i, first, end)
                for s in slots:
                    if tile_due(i, s, X_LAG):
                        pe.wait_ge(xg_in[s], 16 * (i + 1 if s > 0 else i))
                        if tile_past(i, s, X_LAG, 2):
                            pe.wait_ge(xgT_lo, SLOTS * i + s - 2)
                        for c in range(KC):
                            mm = nc.tensor.transpose(ps[:, s % 2, c * P:(c + 1) * P], xg[:, s, c * P:(c + 1) * P], identf)
                        mm.then_inc(xgT_done, 1)
                    if tile_due(i, s, GU_LAG):
                        n = (s - GU_LAG) % 2
                        e = experts[s - GU_LAG]
                        pe.wait_ge(xgT_lo, SLOTS * i + s - GU_LAG)
                        if tile_past(i, s, GU_LAG, 2):
                            pe.wait_ge(h_done, SLOTS * i + s - GU_LAG - 2)
                        for c in range(KC):
                            def w(part):
                                return W[:, bass.ds(e, 1), part, c * F2:(c + 1) * F2].rearrange("p e w -> p (e w)")
                            tok = slice(n * P, n * P + P)
                            mm = mm3(ps[:, 2 + n, :], xT[:, 0, c, tok], xT[:, 1, c, tok], w(0), w(1), c == 0, c == KC - 1)
                        mm.then_inc(gu_done, 1)
                    if tile_due(i, s, H_LAG):
                        n = (s - H_LAG) % 2
                        pe.wait_ge(h_done, SLOTS * i + s - H_LAG)
                        if tile_past(i, s, H_LAG, 2):
                            pe.wait_ge(hT_lo, SLOTS * i + s - H_LAG - 2)
                        for c in range(KC):
                            mm = nc.tensor.transpose(ps[:, 4 + n, c * P:(c + 1) * P], h[:, n, c * P:(c + 1) * P], identf)
                        mm.then_inc(hT_done, 1)
                    if tile_due(i, s, Y_LAG):
                        n = (s - Y_LAG) % 2
                        e = experts[s - Y_LAG]
                        pe.wait_ge(hT_lo, SLOTS * i + s - Y_LAG)
                        if tile_past(i, s, Y_LAG, 2):
                            pe.wait_ge(y_out, SLOTS * i + s - Y_LAG - 2)
                        for c in range(KC):
                            def w(part):
                                at = KC * F2 + c * D
                                return W[:, bass.ds(e, 1), part, at:at + D].rearrange("p e w -> p (e w)")
                            mm = mm3(ps[:, 6 + n, 0:D], rT[:, n, 0, c, :], rT[:, n, 1, c, :], w(0), w(1),
                                     c == 0, c == KC - 1)
                        mm.then_inc(y_done, 1)
            schedule(pe, moe, ROUNDS, Y_LAG)


def kernel(x, ctx_512, g_xattn, g_ffn, L0_xattn_Wq, L0_xattn_Wkv_expand, L0_xattn_Wout, L0_ffn_Wr, L0_ffn_Wg,
           L0_ffn_Wu, L0_ffn_Wd):
    import numpy as np
    import ml_dtypes
    import concourse.bacc as bacc
    from concourse import mybir
    from concourse.bass_utils import run_bass_kernel_spmd

    B, S, D = x.shape
    arrays = {
        "x": np.asarray(x).reshape(B * S, D),
        "ctxT": np.asarray(ctx_512).reshape(B * S, -1).T,
        "g_attn": np.asarray(g_xattn),
        "g_ffn": np.asarray(g_ffn),
        "WqT": np.asarray(L0_xattn_Wq).T,
        "WkvT": np.asarray(L0_xattn_Wkv_expand).T,
        "WoT": np.asarray(L0_xattn_Wout).T,
        "Wr": np.asarray(L0_ffn_Wr),
        "Wgu": np.concatenate([np.asarray(L0_ffn_Wg), np.asarray(L0_ffn_Wu)], axis=2),
        "Wd": np.asarray(L0_ffn_Wd),
    }
    T, E = B * S, L0_ffn_Wr.shape[1]
    NB, K = T // P, 2
    J = K * NB + E
    e, p, tile = np.arange(E), np.arange(P), np.arange(J) - 1

    def rows(a):
        return np.broadcast_to(a.reshape(1, -1), (P, a.size))
    arrays["consts"] = np.concatenate([
        np.eye(P),
        rows(P * np.arange(NB)),
        rows(e[None, :] <= e[:, None]), rows(E - e),
        rows(tile), rows(np.array([D * EPS, D ** 0.5])), p[:, None],
        rows(1 + np.arange(K * NB)),
        P + K * T + P * tile[None, :] + p[:, None],
    ], axis=1).astype(np.float32)
    arrays["consts16"] = np.concatenate(
        [np.where(p[None, :] <= p[:, None], 0.0, MASKED), np.eye(P), p[:, None] < p[None, :], np.ones((P, P)), rows(p)],
        axis=1).astype(ml_dtypes.bfloat16)
    arrays = {n: np.ascontiguousarray(a) for n, a in arrays.items()}
    nc = bacc.Bacc("TRN2", target_bir_lowering=False, num_devices=1)
    args = [nc.dram_tensor(n, a.shape, mybir.dt.from_np(a.dtype), kind="ExternalInput").ap() for n, a in arrays.items()]
    out = nc.dram_tensor("out", (B * S, D), mybir.dt.float32, kind="ExternalOutput").ap()
    build_gated_block(nc, *args, out)
    r = run_bass_kernel_spmd(nc, [arrays], core_ids=[0])
    return r.results[0]["out"].reshape(B, S, D)
```
